# Optimizing a Trainium2 kernel written in Bass

```python
import numpy as np
import jax
import jax.numpy as jnp

def _softmax(x, axis=-1):
    return jax.nn.softmax(x, axis=axis)

def _gelu(x):
    return jax.nn.gelu(x, approximate=True)

def _silu(x):
    return jax.nn.silu(x)

def _sigmoid(x):
    return jax.nn.sigmoid(x)

def _layernorm(x, axis=-1, eps=1e-05):
    m = jnp.mean(x, axis=axis, keepdims=True)
    v = jnp.var(x, axis=axis, keepdims=True)
    return (x - m) / jnp.sqrt(v + eps)

def _scatter_add(tgt, idx, src, axis=0):
    return tgt.at[idx].add(src)

def _segment_sum(src, seg, n):
    return jax.ops.segment_sum(src, seg, n)
kernel_name = 'mk_audio_tower_d1_tok_audfeat256_r4_fec024'

def setup_inputs(seed: int=0):
    np.random.seed(seed)
    _w = jnp.asarray

    def _rec_inputs():
        import jax
        import jax.numpy as jnp
        _rk = jax.random.key(seed)
        x = -0.000392918 + 0.999932 * jax.random.normal(jax.random.fold_in(_rk, 1), (64, 125, 16), jnp.float32)
        return x
    x = _rec_inputs()

    def _L0_tok_setup():
        import jax, jax.numpy as jnp
        import numpy as np
        PATCH = 16
        STRIDE = 8
        EPS = 1e-05
        key = jax.random.key(seed)
        k1, k2, k3 = jax.random.split(key, 3)
        B, S, F, D = (128, 2048, 16, 64)
        in_dim = F * PATCH
        x = jax.random.normal(k1, (B, S, F), dtype=jnp.float32)
        bound = 1.0 / np.sqrt(in_dim)
        W = jax.random.uniform(k2, (D, in_dim), minval=-bound, maxval=bound, dtype=jnp.float32)
        b = jax.random.uniform(k3, (D,), minval=-bound, maxval=bound, dtype=jnp.float32)
        gamma = jnp.ones((D,), dtype=jnp.float32)
        beta = jnp.zeros((D,), dtype=jnp.float32)
        return {'x': x, 'W': W, 'b': b, 'gamma': gamma, 'beta': beta}
    _L0_tok_all = _L0_tok_setup()
    _L0_tok_in = {k: v for k, v in _L0_tok_all.items() if k in ('W', 'b', 'gamma', 'beta')}
    del _L0_tok_all

    def _L0_attn_setup():
        import jax, jax.numpy as jnp
        import numpy as np
        B, S, F, H = (4, 256, 64, 8)
        SCALE = float(F) ** 0.5
        key = jax.random.key(seed)
        ks = jax.random.split(key, 5)
        return {'q_input': jax.random.normal(ks[0], (B, S, F), dtype=jnp.float32), 'Wq': jax.random.normal(ks[1], (F, F * H), dtype=jnp.float32) * 0.02, 'Wk': jax.random.normal(ks[2], (F, F * H), dtype=jnp.float32) * 0.02, 'Wv': jax.random.normal(ks[3], (F, F * H), dtype=jnp.float32) * 0.02, 'Wo': jax.random.normal(ks[4], (F * H, F), dtype=jnp.float32) * 0.02}
    _L0_attn_all = _L0_attn_setup()
    _L0_attn_in = {k: v for k, v in _L0_attn_all.items() if k in ('Wq', 'Wk', 'Wv', 'Wo')}
    del _L0_attn_all

    def _L0_ffn_setup():
        import jax, jax.numpy as jnp
        import numpy as np
        B, S, H, F, E, K = (8, 1024, 64, 128, 16, 2)
        EPS = 1e-05
        key = jax.random.key(seed)
        ks = jax.random.split(key, 9)
        sc = 0.02
        return {'x': jax.random.normal(ks[0], (B, S, H), dtype=jnp.float32), 'gate_w': jax.random.normal(ks[1], (H, E), dtype=jnp.float32) * sc, 'gate_b': jnp.zeros((E,), dtype=jnp.float32), 'w1': jax.random.normal(ks[2], (E, H, F), dtype=jnp.float32) * sc, 'b1': jnp.zeros((E, F), dtype=jnp.float32), 'w2': jax.random.normal(ks[3], (E, F, H), dtype=jnp.float32) * sc, 'b2': jnp.zeros((E, H), dtype=jnp.float32), 'gamma': jnp.ones((H,), dtype=jnp.float32), 'beta': jnp.zeros((H,), dtype=jnp.float32)}
    _L0_ffn_all = _L0_ffn_setup()
    _L0_ffn_in = {k: v for k, v in _L0_ffn_all.items() if k in ('gate_w', 'gate_b', 'w1', 'b1', 'w2', 'b2', 'gamma', 'beta')}
    del _L0_ffn_all
    return {'x': x, 'L0_tok_W': _L0_tok_in['W'], 'L0_tok_b': _L0_tok_in['b'], 'L0_tok_gamma': _L0_tok_in['gamma'], 'L0_tok_beta': _L0_tok_in['beta'], 'L0_attn_Wq': _L0_attn_in['Wq'], 'L0_attn_Wk': _L0_attn_in['Wk'], 'L0_attn_Wv': _L0_attn_in['Wv'], 'L0_attn_Wo': _L0_attn_in['Wo'], 'L0_ffn_gate_w': _L0_ffn_in['gate_w'], 'L0_ffn_gate_b': _L0_ffn_in['gate_b'], 'L0_ffn_w1': _L0_ffn_in['w1'], 'L0_ffn_b1': _L0_ffn_in['b1'], 'L0_ffn_w2': _L0_ffn_in['w2'], 'L0_ffn_b2': _L0_ffn_in['b2'], 'L0_ffn_gamma': _L0_ffn_in['gamma'], 'L0_ffn_beta': _L0_ffn_in['beta']}

def reference(x, L0_tok_W, L0_tok_b, L0_tok_gamma, L0_tok_beta, L0_attn_Wq, L0_attn_Wk, L0_attn_Wv, L0_attn_Wo, L0_ffn_gate_w, L0_ffn_gate_b, L0_ffn_w1, L0_ffn_b1, L0_ffn_w2, L0_ffn_b2, L0_ffn_gamma, L0_ffn_beta):
    import jax
    import jax.numpy as jnp

    def _L0_tok_ref(x, W, b, gamma, beta):
        import jax, jax.numpy as jnp
        import numpy as np
        PATCH = 16
        STRIDE = 8
        EPS = 1e-05
        B, S, F = x.shape
        starts = jnp.arange(0, S - PATCH + 1, STRIDE)
        idx = starts[:, None] + jnp.arange(PATCH)[None, :]
        patches = x[:, idx, :].reshape(B, idx.shape[0], PATCH * F)
        y = jnp.einsum('bpi,di->bpd', patches, W) + b
        mu = jnp.mean(y, axis=-1, keepdims=True)
        var = jnp.mean(jnp.square(y - mu), axis=-1, keepdims=True)
        return (y - mu) * jax.lax.rsqrt(var + EPS) * gamma + beta

    def _L0_attn_ref(q_input, Wq, Wk, Wv, Wo):
        import jax, jax.numpy as jnp
        import numpy as np
        B, S, F, H = (4, 256, 64, 8)
        SCALE = float(F) ** 0.5
        b, s, f = q_input.shape
        h = Wq.shape[1] // f
        q = (q_input.reshape(b * s, f) @ Wq).reshape(b, s, f, h)
        k = (q_input.reshape(b * s, f) @ Wk).reshape(b, s, f, h)
        v = (q_input.reshape(b * s, f) @ Wv).reshape(b, s, f, h)
        qkt = jnp.einsum('bifh,bjfh->bijh', q, k)
        attn = jax.nn.sigmoid(qkt * SCALE)
        wv = jnp.einsum('bijh,bjfh->bifh', attn, v)
        wv = wv.reshape(b * s, f * h)
        out = jax.nn.relu(wv @ Wo)
        return out.reshape(b, s, f)

    def _L0_ffn_ref(x, gate_w, gate_b, w1, b1, w2, b2, gamma, beta):
        import jax, jax.numpy as jnp
        import numpy as np
        B, S, H, F, E, K = (8, 1024, 64, 128, 16, 2)
        EPS = 1e-05
        gate_logits = x @ gate_w + gate_b
        topk_vals, topk_idx = jax.lax.top_k(gate_logits, K)
        topk_w = jax.nn.softmax(topk_vals, axis=-1)
        h = jax.nn.relu(jnp.einsum('bsh,ehf->bsef', x, w1) + b1)
        expert_out = jnp.einsum('bsef,efh->bseh', h, w2) + b2
        sel = jnp.take_along_axis(expert_out, topk_idx[:, :, :, None], axis=2)
        moe = jnp.sum(topk_w[..., None] * sel, axis=2)
        y = x + moe
        mu = jnp.mean(y, axis=-1, keepdims=True)
        var = jnp.var(y, axis=-1, keepdims=True)
        return (y - mu) / jnp.sqrt(var + EPS) * gamma + beta
    h = _L0_tok_ref(x, L0_tok_W, L0_tok_b, L0_tok_gamma, L0_tok_beta)
    h = h + _L0_attn_ref(_layernorm(h, axis=-1), L0_attn_Wq, L0_attn_Wk, L0_attn_Wv, L0_attn_Wo)
    h = h + _L0_ffn_ref(_layernorm(h, axis=-1), L0_ffn_gate_w, L0_ffn_gate_b, L0_ffn_w1, L0_ffn_b1, L0_ffn_w2, L0_ffn_b2, L0_ffn_gamma, L0_ffn_beta)
    return h

_drawn_inputs = setup_inputs


def setup_inputs(seed=0):
    import zlib

    import numpy as np

    out = dict(_drawn_inputs(seed))
    spreads = {'L0_tok_gamma': (1.0, 0.2),
     'L0_tok_beta': (0.0, 0.1),
     'L0_ffn_gate_b': (0.0, 0.1),
     'L0_ffn_b1': (0.0, 0.8),
     'L0_ffn_b2': (0.0, 0.299),
     'L0_ffn_gamma': (1.0, 0.2),
     'L0_ffn_beta': (0.0, 0.1)}
    factors = {'L0_ffn_w1': 7.414, 'L0_ffn_w2': 5.584}
    for name, (base, spread) in spreads.items():
        noise = np.random.default_rng([zlib.crc32(name.encode()), seed]).standard_normal(out[name].shape)
        drawn = base * np.exp(spread * noise) if base else spread * noise
        out[name] = jnp.asarray(drawn.astype(out[name].dtype))
    for name, factor in factors.items():
        out[name] = (out[name] * factor).astype(out[name].dtype)
    return out
```

```python
from contextlib import ExitStack

import concourse.bass as bass
from concourse import mybir

B, S, FEAT = 64, 125, 16
PATCH, STRIDE = 16, 8
P = (S - PATCH) // STRIDE + 1
D, H, E, F = 64, 8, 16, 128
C = STRIDE * FEAT
Q = P + PATCH // STRIDE - 1
TOK = B * P
T = 112
NT = TOK // T
BT = T // P
HALVES = 2
TH = NT // HALVES
N = TH * T
QUADS = 4
W = T // QUADS
PAD = 32
HP = H // 2
EP = E // 2
EPS = 1e-5
BIG = -3.0e38


def audio_tower(nc, x, tok_w, tok_b, tok_gamma, tok_beta, wq, wk, wv, wo, gate_w, gate_b, w1, b1, w2, b2,
                ffn_gamma, ffn_beta, c_main, c_sel, out):
    F32, F32R = mybir.dt.float32, mybir.dt.float32r
    ALU, ACT, AX = mybir.AluOpType, mybir.ActivationFunctionType, mybir.AxisListType

    ctx = ExitStack()
    with ctx:
        def sb(name, shape, dt=F32):
            return ctx.enter_context(nc.sbuf_tensor(name, shape, dt))

        def sem(name):
            return ctx.enter_context(nc.semaphore(name))

        def f32(ap):
            return ap.bitcast(F32)

        cst = sb("cst", [128, 128 + D + W + E])
        ident, idup = cst[:, 0:128], cst[:, 128:128 + D]
        mask, rank = cst[:, 192:192 + W], cst[:, 192 + W:192 + W + E]
        sel_raw = sb("sel_raw", [2 * E, EP * 128])
        sel = sb("sel", [2 * E, EP * 128], F32R)
        xb = sb("xb", [B, Q * C])
        w_raw = sb("w_raw", [D, 2 * C])
        wq_raw = sb("wq_raw", [128, H * D])
        wk_raw = sb("wk_raw", [D, H * D])
        wv_raw = sb("wv_raw", [128, H * D])
        wo_sb = sb("wo_sb", [128, HP, D])
        rows = sb("rows", [T, 5, D])
        tokb, tokg, tokbe, ffng, ffnbe = (rows[:, i, :] for i in range(5))
        gateb = sb("gateb", [T, E])
        b12_raw = sb("b12_raw", [E + EP, 128])
        gw_raw = sb("gw_raw", [128, E])
        w1_raw = sb("w1_raw", [128, E, F])
        w2_sb = sb("w2_sb", [128, E, D])
        tokwT = sb("tokwT", [128, 2, D])
        wq_h = sb("wq_h", [128, H, D])
        wk_h = sb("wk_h", [D, H, D])
        wv_h = sb("wv_h", [128, H, D])
        fold = sb("fold", [128, 2, D], F32R)
        wqT = sb("wqT", [128, HP, 128])
        wkT = sb("wkT", [128, HP, D])
        wvT = sb("wvT", [128, HP, 128])
        a_hi, a_lo = sb("a_hi", [128, HP, 2, D], F32R), sb("a_lo", [128, HP, 2, D], F32R)
        b_hi, b_lo = sb("b_hi", [128, HP, 2, D], F32R), sb("b_lo", [128, HP, 2, D], F32R)
        b12T = sb("b12T", [128, E + EP])
        gw_hi, gw_lo = sb("gw_hi", [128, E], F32R), sb("gw_lo", [128, E], F32R)
        w1_hi, w1_lo = sb("w1_hi", [128, E, F], F32R), sb("w1_lo", [128, E, F], F32R)
        xT = sb("xT", [128, 2, B, P])
        yb = sb("yb", [T, NT, D])
        h0 = sb("h0", [T, NT, D])
        h1 = sb("h1", [T, NT, D])
        xn = sb("xn", [T, NT, D])
        xn2 = sb("xn2", [T, NT, D])
        y2 = sb("y2", [T, NT, D])
        h1b = sb("h1b", [T, NT, D])
        res = sb("res", [T, NT, D])
        stack = sb("stack", [T, NT, 2, D], F32R)
        stack2 = sb("stack2", [T, NT, 2, D], F32R)
        stats = sb("stats", [T, 4, NT, 6])
        mv = sb("mv", [T, 4, NT, 2])
        var = sb("var", [T, 4, NT])
        rstd = sb("rstd", [T, 4, NT])
        mhalf = sb("mhalf", [T, NT])
        xs = sb("xs", [128, NT * QUADS, PAD], F32R)
        xff = sb("xff", [128, NT * QUADS, PAD])
        tT = sb("tT", [128, HP, TOK])
        u = sb("u", [128, NT, H * D])
        att = sb("att", [128, HALVES, 2 * TH * HP, W])
        bd = sb("bd", [128, HALVES, 2 * TH * HP, QUADS, W])
        oT = sb("oT", [128, HALVES, TH // 2 * T])
        xs2 = sb("xs2", [128, TOK], F32R)
        lg = sb("lg", [T, HALVES, TH, E])
        lg2 = sb("lg2", [T, HALVES, TH, E])
        eq = sb("eq", [T, HALVES, TH, E])
        one1 = sb("one1", [T, HALVES, TH, E])
        one2 = sb("one2", [T, HALVES, TH, E])
        g = sb("g", [T, HALVES, TH, E])
        top = sb("top", [T, HALVES, 7, TH])
        gs = sb("gs", [T, HALVES, TH, 2 * E], F32R)
        gT = sb("gT", [2 * E, TOK], F32R)
        h1e = sb("h1e", [128, 2, 2, N])
        gbc = sb("gbc", [128, 2, N])
        xT_flat = xT[:, :, :, :].rearrange("c k b p -> c (k b p)")
        part = xT_flat[:, 0:2 * N].rearrange("p (i n) -> p i n", n=N)
        acc = xT_flat[:, 2 * N:4 * N].rearrange("p (i n) -> p i n", n=N)

        bank = [ctx.enter_context(nc.psum_tensor(f"bank{i}", [128, 512], F32)) for i in range(8)]

        ld_x = [sem(f"ld_x{i}") for i in range(2)]
        ld_c, ld_tokw, ld_rows, ld_wqk, ld_wvo = (sem(n) for n in ("ld_c", "ld_tokw", "ld_rows", "ld_wqk", "ld_wvo"))
        ld_b12, ld_gw, ld_w1, ld_w2, ld_sel = (sem(n) for n in ("ld_b12", "ld_gw", "ld_w1", "ld_w2", "ld_sel"))
        stored = sem("stored")
        names = ("pe_tokwT", "pe_xT", "pe_wkT", "pe_wqT", "pe_wvT", "pe_y", "pe_a", "pe_b", "pe_xs", "pe_xff", "pe_t", "pe_u",
                 "pe_s", "pe_av", "pe_oT", "pe_xs2", "pe_lg", "pe_gT", "pe_z", "pe_g", "pe_o", "pe_fin")
        (pe_tokwT, pe_xT, pe_wkT, pe_wqT, pe_wvT, pe_y, pe_a, pe_b, pe_xs, pe_xff, pe_t, pe_u,
         pe_s, pe_av, pe_oT, pe_xs2, pe_lg, pe_gT, pe_z, pe_g, pe_o, pe_fin) = (sem(n) for n in names)
        names = ("act_tokwT", "act_xT", "act_wkT", "act_wqT", "act_wvT", "act_a", "act_b", "act_w1", "act_hi",
                 "act_xs", "act_t", "act_u", "act_sig", "act_bd", "act_oT", "act_hi2", "act_xs2", "act_top", "act_gT",
                 "act_z", "act_g", "act_sel", "act_gw", "act_wh")
        (act_tokwT, act_xT, act_wkT, act_wqT, act_wvT, act_a, act_b, act_w1, act_hi,
         act_xs, act_t, act_u, act_sig, act_bd, act_oT, act_hi2, act_xs2, act_top, act_gT,
         act_z, act_g, act_sel, act_gw, act_wh) = (sem(n) for n in names)
        names = ("dve_link", "dve_zero", "dve_xT", "dve_y", "dve_var", "dve_xn", "dve_lo", "dve_a", "dve_b", "dve_xff",
                 "dve_t", "dve_u", "dve_mask", "dve_bd", "dve_h1", "dve_xn2", "dve_lo2", "dve_lg", "dve_gap",
                 "dve_gate", "dve_z", "dve_part", "dve_out", "dve_gw", "dve_fold", "dve_wh")
        (dve_link, dve_zero, dve_xT, dve_y, dve_var, dve_xn, dve_lo, dve_a, dve_b, dve_xff,
         dve_t, dve_u, dve_mask, dve_bd, dve_h1, dve_xn2, dve_lo2, dve_lg, dve_gap,
         dve_gate, dve_z, dve_part, dve_out, dve_gw, dve_fold, dve_wh) = (sem(n) for n in names)
        pool_pads, pool_bd, pool_half, pool_rstd, pool_w1, pool_acc, pool_h1b = (
            sem(n) for n in ("pool_pads", "pool_bd", "pool_half", "pool_rstd", "pool_w1", "pool_acc", "pool_h1b"))

        block = ctx.enter_context(nc.Block())

        def tiles(h):
            return range(h * TH, (h + 1) * TH)

        def half(ap, h):
            return ap[:, h * TH:(h + 1) * TH, :]

        STEPS = [(h, p) for h in range(HALVES) for p in range(EP)]

        @block.sync
        def _(sp):
            xv = x.rearrange("b s f -> b (s f)")
            sp.dma_start(xb[:, 0:8 * C], xv[:, 0:8 * C]).then_inc(ld_x[0], 16)
            sp.dma_start(xb[:, 8 * C:], xv[:, 8 * C:Q * C]).then_inc(ld_x[1], 16)
            wov = wo.rearrange("(f p two) n -> two f p n", two=2, p=HP)
            for r in range(2):
                sp.dma_start(wq_raw[r * D:(r + 1) * D, :], wq).then_inc(ld_wqk, 16)
            for r in range(2):
                sp.dma_start(wo_sb[r * D:(r + 1) * D, :, :], wov[r]).then_inc(ld_wvo, 16)
            for r in range(2):
                sp.dma_start(gw_raw[r * D:(r + 1) * D, :], gate_w).then_inc(ld_gw, 16)
            for r in range(2):
                sp.dma_start(w1_raw[r * D:(r + 1) * D, :, :], w1.rearrange("e d f -> d e f")).then_inc(ld_w1, 16)
            sp.dma_start(w2_sb[:, :, :], w2.rearrange("e f d -> f e d")).then_inc(ld_w2, 16)
            ov = out.rearrange("b p d -> (b p) d").rearrange("(t p) d -> p t d", p=T)
            for h in range(HALVES):
                sp.wait_ge(dve_out, h + 1)
                sp.dma_start(ov[:, h * TH:(h + 1) * TH, :], half(res, h)).then_inc(stored, 16)
            sp.wait_ge(stored, 16 * HALVES)

        @block.gpsimd
        def _(pool):
            nc.gpsimd.memset(mhalf[:, :], -0.5).then_inc(pool_half, 1)
            nc.gpsimd.memset(f32(xs[:, :, :]), 0.0).then_inc(pool_pads, 1)
            nc.gpsimd.memset(bd[:, 0, :, :, :], 0.0).then_inc(pool_bd, 1)

            def inverse_root(n, h, count):
                pool.wait_ge(dve_var, count)
                nc.gpsimd.tensor_tensor(rstd[:, n, h * TH:(h + 1) * TH], var[:, n, h * TH:(h + 1) * TH],
                                        mhalf[:, h * TH:(h + 1) * TH], ALU.pow).then_inc(pool_rstd, 1)

            pool.wait_ge(pool_half, 1)
            for n in range(2):
                for h in range(HALVES):
                    inverse_root(n, h, 2 * n + h + 1)
            pool.wait_ge(act_w1, 1)
            for c in range(4):
                r = slice(c * E // 4, (c + 1) * E // 4)
                nc.gpsimd.tensor_tensor(w1_lo[:, r, :], w1_raw[:, r, :], f32(w1_hi[:, r, :]),
                                        ALU.subtract).then_inc(pool_w1, 1)
            for h in range(HALVES):
                inverse_root(2, h, 4 + h + 1)
            for h in range(HALVES):
                pool.wait_ge(dve_h1, h + 1)
                nc.gpsimd.tensor_tensor(half(h1b, h), half(h1, h), ffnbe.unsqueeze(1).broadcast_to([T, TH, D]),
                                        ALU.add).then_inc(pool_h1b, 1)
            for k, (h, p) in enumerate(STEPS):
                if 0 < p < EP - 1:
                    pool.wait_ge(dve_part, k + 1)
                    if p > 1:
                        pool.wait_ge(pool_acc, h * (EP - 2) + p - 1)
                    nc.gpsimd.tensor_tensor(acc[:, h, :], acc[:, h, :], part[:, k % 2, :],
                                            ALU.add).then_inc(pool_acc, 1)
                if h == 1 and p == 2:
                    inverse_root(3, 0, 7)
            inverse_root(3, 1, 8)

        @block.scalar
        def _(act):
            act.dma_start(cst[:, :], c_main).then_inc(ld_c, 16)
            act.dma_start(w_raw[:, :], tok_w).then_inc(ld_tokw, 16)
            act.dma_start(wk_raw[:, :], wk).then_inc(ld_wqk, 16)
            for i, v in enumerate((tok_b, tok_gamma, tok_beta, ffn_gamma, ffn_beta)):
                act.dma_start(rows[:, i, :], v.unsqueeze(0).broadcast_to([T, D])).then_inc(ld_rows, 16)
            for r in range(2):
                act.dma_start(wv_raw[r * D:(r + 1) * D, :], wv).then_inc(ld_wvo, 16)
            act.dma_start(b12_raw[0:E, :], b1).then_inc(ld_b12, 16)
            act.dma_start(b12_raw[E:E + EP, :], b2.rearrange("(p two) d -> p (two d)", two=2)).then_inc(ld_b12, 16)
            act.dma_start(sel_raw[:, :], c_sel).then_inc(ld_sel, 16)
            act.dma_start(gateb[:, :], gate_b.unsqueeze(0).broadcast_to([T, E])).then_inc(ld_rows, 16)

            act.wait_ge(pe_tokwT, 1)
            nc.scalar.copy(tokwT[:, :, :], bank[3][:, 0:2 * D]).then_inc(act_tokwT, 1)
            act.wait_ge(ld_wqk, 48)
            nc.scalar.copy(wq_h[:, :, :], wq_raw[:, :].rearrange("r (f h) -> r h f", h=H)).then_inc(act_wh, 1)
            act.wait_ge(pe_xT, 1)
            v = bank[0][:, 0:8 * B].rearrange("p (q b) -> p b q", b=B)
            nc.scalar.copy(xT[:, 0, :, 0:8], v)
            nc.scalar.copy(xT[:, 1, :, 0:7], v[:, :, 1:8]).then_inc(act_xT, 1)
            act.wait_ge(ld_wvo, 64)
            nc.scalar.copy(wv_h[:, :, :], wv_raw[:, :].rearrange("r (f h) -> r h f", h=H)).then_inc(act_wh, 1)
            act.wait_ge(pe_wkT, 1)
            nc.scalar.copy(wkT[:, :, :], bank[5][:, 0:HP * D])
            nc.scalar.copy(b12T[:, :], bank[5][:, HP * D:HP * D + E + EP]).then_inc(act_wkT, 1)
            act.wait_ge(pe_wqT, 1)
            nc.scalar.copy(wqT[:, :, :], bank[4][:, :]).then_inc(act_wqT, 1)
            act.wait_ge(pe_wvT, 1)
            nc.scalar.copy(wvT[:, :, :], bank[6][:, :]).then_inc(act_wvT, 1)
            for par, bk in enumerate((7, 0)):
                act.wait_ge(pe_a, par + 1)
                nc.scalar.copy(a_hi[:, :, par, :], bank[bk][:, 0:HP * D].rearrange("p (a d) -> p a d", d=D)
                               ).then_inc(act_a, 1)
            for par, bk in enumerate((1, 6)):
                act.wait_ge(pe_b, par + 1)
                nc.scalar.copy(b_hi[:, :, par, :], bank[bk][:, 0:HP * D].rearrange("p (a d) -> p a d", d=D)
                               ).then_inc(act_b, 1)

            def high_part(dst, src, ready, signal, h):
                act.wait_ge(ready, h + 1)
                nc.scalar.copy(dst[:, h * TH:(h + 1) * TH, 0, :], half(src, h)).then_inc(signal, 1)

            high_part(stack, xn, dve_xn, act_hi, 0)
            act.wait_ge(ld_gw, 32)
            nc.scalar.copy(gw_hi[:, :], gw_raw[:, :]).then_inc(act_gw, 1)
            act.wait_ge(ld_w1, 32)
            nc.scalar.copy(w1_hi[:, :, :], w1_raw[:, :, :]).then_inc(act_w1, 1)
            high_part(stack, xn, dve_xn, act_hi, 1)

            T_BANK = ((0, 1, 6, 7), (6, 7, 3, 5))
            U_BANK = ((2, 3, 4, 5), (2, 4, 6, 7))
            S_BANK = ((0, 1), (1, 3))

            def move_xs(h):
                act.wait_ge(pool_pads, 1)
                act.wait_ge(pe_xs, h + 1)
                nc.scalar.copy(xs[:, h * TH * QUADS:(h + 1) * TH * QUADS, 0:W],
                               bank[2][:, 0:N].rearrange("p (q w) -> p q w", w=W)).then_inc(act_xs, 1)

            def move_t(h):
                for p in (0, 2):
                    act.wait_ge(pe_t, HP * h + p + 1)
                    nc.scalar.copy(tT[:, p, h * N:(h + 1) * N], bank[T_BANK[h][p]][:, 0:N]).then_inc(act_t, 1)

            def move_u(h):
                for i in (0, 2):
                    act.wait_ge(pe_u, TH * h + i + 1)
                    nc.scalar.copy(u[:, h * TH + i, :], bank[U_BANK[h][i]][:, :]).then_inc(act_u, 1)

            def sigmoids(h):
                for par in range(2):
                    act.wait_ge(pe_s, 2 * h + par + 1)
                    nc.scalar.activation(att[:, h, par * TH * HP:(par + 1) * TH * HP, :],
                                         bank[S_BANK[h][par]][:, 0:N].rearrange("p (a w) -> p a w", w=W),
                                         ACT.Sigmoid, scale=float(D) ** 0.5).then_inc(act_sig, 1)

            def expand(h):
                act.wait_ge(dve_mask, h + 1)
                if h == 0:
                    act.wait_ge(pool_bd, 1)
                else:
                    act.wait_ge(dve_zero, 1)
                for q in (0, 1):
                    nc.scalar.copy(bd[q * PAD:(q + 1) * PAD, h, :, q, :],
                                   att[q * PAD:(q + 1) * PAD, h, :, :]).then_inc(act_bd, 1)

            def move_av(h):
                act.wait_ge(pe_av, h + 1)
                nc.scalar.activation(oT[:, h, :], bank[h][:, 0:TH // 2 * T], ACT.Relu).then_inc(act_oT, 1)

            def move_xs2(h):
                act.wait_ge(pe_xs2, h + 1)
                nc.scalar.copy(xs2[:, h * N:(h + 1) * N], bank[(0, 5)[h]][:, 0:N]).then_inc(act_xs2, 1)

            def gate_weights(h):
                act.wait_ge(dve_gap, h + 1)
                nc.scalar.activation(top[:, h, 5, :], top[:, h, 4, :], ACT.Sigmoid, scale=-1.0)
                nc.scalar.activation(top[:, h, 6, :], top[:, h, 4, :], ACT.Sigmoid).then_inc(act_top, 1)

            move_xs(0)
            move_t(0)
            move_u(0)
            move_xs(1)
            sigmoids(0)
            expand(0)
            move_t(1)
            move_u(1)
            move_av(0)
            sigmoids(1)
            expand(1)
            high_part(stack2, xn2, dve_xn2, act_hi2, 0)
            move_xs2(0)
            move_av(1)
            act.wait_ge(ld_sel, 16)
            nc.scalar.copy(sel[:, :], sel_raw[:, :]).then_inc(act_sel, 1)
            gate_weights(0)
            high_part(stack2, xn2, dve_xn2, act_hi2, 1)
            move_xs2(1)

            def move_gT(h):
                act.wait_ge(pe_gT, h + 1)
                nc.scalar.copy(gT[:, h * N:(h + 1) * N], bank[(4, 7)[h]][0:2 * E, 0:N]).then_inc(act_gT, 1)

            move_gT(0)
            for k, (h, p) in enumerate(STEPS):
                if k == 3:
                    gate_weights(1)
                if k == 7:
                    move_gT(1)
                act.wait_ge(pe_z, 2 * k + 1)
                if k >= 2:
                    act.wait_ge(pe_o, k - 1)
                nc.scalar.activation(h1e[:, k % 2, 0, :], bank[2 * (k % 2)][:, 0:N], ACT.Relu,
                                     bias=b12T[:, 2 * p:2 * p + 1]).then_inc(act_z, 1)
                act.wait_ge(pe_g, k + 1)
                if k >= 2:
                    act.wait_ge(dve_part, k - 1)
                nc.scalar.copy(gbc[:, k % 2, :], bank[6][:, 0:N]).then_inc(act_g, 1)

        @block.vector
        def _(dve):
            made = [0]

            def link(ins):
                made[0] += 1
                ins.then_inc(dve_link, 1)
                dve.wait_ge(dve_link, made[0])

            def bcast(row):
                return row.unsqueeze(1).broadcast_to([T, TH, row.shape[-1]])

            def statistics(n, src, h):
                for t in tiles(h):
                    last = nc.vector.bn_stats(stats[:, n, t, :], src[:, t, :])
                link(last)
                for t in tiles(h):
                    last = nc.vector.bn_aggr(mv[:, n, t, :], stats[:, n, t, :])
                link(last)
                nc.vector.tensor_scalar(var[:, n, h * TH:(h + 1) * TH], mv[:, n, h * TH:(h + 1) * TH, 1], EPS, None,
                                        ALU.add).then_inc(dve_var, 1)

            def normalise(n, dst, src, h):
                dve.wait_ge(pool_rstd, 2 * n + h + 1)
                for t in tiles(h):
                    last = nc.vector.tensor_scalar(dst[:, t, :], src[:, t, :], mv[:, n, t, 0:1],
                                                   rstd[:, n, t:t + 1], ALU.subtract, ALU.mult)
                return last

            nc.vector.memset(bd[:, 1, :, :, :], 0.0).then_inc(dve_zero, 1)
            dve.wait_ge(ld_c, 16)
            nc.vector.tensor_copy(fold[:, :, :], idup.unsqueeze(1).broadcast_to([128, 2, D])).then_inc(dve_fold, 1)
            dve.wait_ge(pe_xT, 2)
            v = bank[1][:, 0:(Q - 8) * B].rearrange("p (q b) -> p b q", b=B)
            nc.vector.tensor_copy(xT[:, 0, :, 8:P], v[:, :, 0:P - 8])
            nc.vector.tensor_copy(xT[:, 1, :, 7:P], v).then_inc(dve_xT, 1)
            dve.wait_ge(ld_wqk, 48)
            nc.vector.tensor_copy(wk_h[:, :, :], wk_raw[:, :].rearrange("r (f h) -> r h f", h=H)).then_inc(dve_wh, 1)
            dve.wait_ge(ld_rows, 16 * 6)
            for h in range(HALVES):
                dve.wait_ge(pe_y, h + 1)
                nc.vector.tensor_tensor(half(yb, h), bank[2 + h][0:T, 0:TH * D].rearrange("p (t d) -> p t d", d=D),
                                        bcast(tokb), ALU.add).then_inc(dve_y, 1)
                dve.wait_ge(dve_y, h + 1)
                statistics(0, yb, h)
            for h in range(HALVES):
                link(normalise(0, yb, yb, h))
                link(nc.vector.tensor_tensor(half(yb, h), half(yb, h), bcast(tokg), ALU.mult))
                link(nc.vector.tensor_tensor(half(h0, h), half(yb, h), bcast(tokbe), ALU.add))
                statistics(1, h0, h)
            for par, bk in enumerate((7, 0)):
                dve.wait_ge(act_a, par + 1)
                nc.vector.tensor_tensor(a_lo[:, :, par, :], bank[bk][:, 0:HP * D].rearrange("p (a d) -> p a d", d=D),
                                        f32(a_hi[:, :, par, :]), ALU.subtract).then_inc(dve_a, 1)
            for h in range(HALVES):
                normalise(1, xn, h0, h).then_inc(dve_xn, 1)
                if h == 0:
                    for par, bk in enumerate((1, 6)):
                        dve.wait_ge(act_b, par + 1)
                        nc.vector.tensor_tensor(b_lo[:, :, par, :],
                                                bank[bk][:, 0:HP * D].rearrange("p (a d) -> p a d", d=D),
                                                f32(b_hi[:, :, par, :]), ALU.subtract).then_inc(dve_b, 1)
                dve.wait_ge(act_hi, h + 1)
                dve.wait_ge(dve_xn, h + 1)
                nc.vector.tensor_tensor(stack[:, h * TH:(h + 1) * TH, 1, :], half(xn, h),
                                        f32(stack[:, h * TH:(h + 1) * TH, 0, :]), ALU.subtract).then_inc(dve_lo, 1)

            T_BANK = ((0, 1, 6, 7), (6, 7, 3, 5))
            U_BANK = ((2, 3, 4, 5), (2, 4, 6, 7))

            def move_xff(h):
                dve.wait_ge(pe_xff, h + 1)
                nc.vector.tensor_copy(xff[:, h * TH * QUADS:(h + 1) * TH * QUADS, :],
                                      bank[4][:, :]).then_inc(dve_xff, 1)

            def move_t(h):
                for p in (1, 3):
                    dve.wait_ge(pe_t, HP * h + p + 1)
                    nc.vector.tensor_copy(tT[:, p, h * N:(h + 1) * N], bank[T_BANK[h][p]][:, 0:N]).then_inc(dve_t, 1)

            def move_u(h):
                for i in (1, 3):
                    dve.wait_ge(pe_u, TH * h + i + 1)
                    nc.vector.tensor_copy(u[:, h * TH + i, :], bank[U_BANK[h][i]][:, :]).then_inc(dve_u, 1)

            def mask_and_expand(h):
                dve.wait_ge(act_sig, 2 * h + 2)
                nc.vector.tensor_tensor(att[:, h, :, :], att[:, h, :, :],
                                        mask.unsqueeze(1).broadcast_to([128, 2 * TH * HP, W]),
                                        ALU.mult).then_inc(dve_mask, 1)
                dve.wait_ge(dve_mask, h + 1)
                if h == 0:
                    dve.wait_ge(pool_bd, 1)
                for q in (2, 3):
                    nc.vector.tensor_copy(bd[q * PAD:(q + 1) * PAD, h, :, q, :],
                                          att[q * PAD:(q + 1) * PAD, h, :, :]).then_inc(dve_bd, 1)

            def residual(h):
                dve.wait_ge(pe_oT, h + 1)
                nc.vector.tensor_tensor(half(h1, h), bank[(5, 3)[h]][0:T, 0:TH * D].rearrange("p (t d) -> p t d", d=D),
                                        half(h0, h), ALU.add).then_inc(dve_h1, 1)
                dve.wait_ge(dve_h1, h + 1)
                statistics(2, h1, h)

            def second_norm(h):
                normalise(2, xn2, h1, h).then_inc(dve_xn2, 1)

            def low_part(h):
                dve.wait_ge(act_hi2, h + 1)
                dve.wait_ge(dve_xn2, h + 1)
                nc.vector.tensor_tensor(stack2[:, h * TH:(h + 1) * TH, 1, :], half(xn2, h),
                                        f32(stack2[:, h * TH:(h + 1) * TH, 0, :]), ALU.subtract).then_inc(dve_lo2, 1)

            def wide(col):
                return col.unsqueeze(2).broadcast_to([T, TH, E])

            def pick(logits, hot, h, m, k):
                link(nc.vector.reduce_max(top[:, h, m, :], logits[:, h, :, :], AX.X))
                link(nc.vector.tensor_tensor(eq[:, h, :, :], logits[:, h, :, :], wide(top[:, h, m, :]), ALU.is_equal))
                link(nc.vector.tensor_tensor(eq[:, h, :, :], eq[:, h, :, :], bcast(rank[0:T, :]), ALU.mult))
                link(nc.vector.reduce_max(top[:, h, k, :], eq[:, h, :, :], AX.X))
                link(nc.vector.tensor_tensor(hot[:, h, :, :], eq[:, h, :, :], wide(top[:, h, k, :]), ALU.is_equal))

            def gates(h):
                dve.wait_ge(pe_lg, h + 1)
                nc.vector.tensor_tensor(lg[:, h, :, :], bank[(2, 7)[h]][0:T, 0:TH * E].rearrange(
                    "p (t e) -> p t e", e=E), bcast(gateb[:, :]), ALU.add).then_inc(dve_lg, 1)
                dve.wait_ge(dve_lg, h + 1)
                pick(lg, one1, h, 0, 1)
                link(nc.vector.scalar_tensor_tensor(out=lg2[:, h, :, :], in0=one1[:, h, :, :], scalar=BIG,
                                                    in1=lg[:, h, :, :], op0=ALU.mult, op1=ALU.add))
                pick(lg2, one2, h, 2, 3)
                nc.vector.tensor_tensor(top[:, h, 4, :], top[:, h, 2, :], top[:, h, 0, :],
                                        ALU.subtract).then_inc(dve_gap, 1)

            def spread_gates(h):
                dve.wait_ge(act_top, h + 1)
                nc.vector.tensor_tensor(one1[:, h, :, :], one1[:, h, :, :], wide(top[:, h, 5, :]), ALU.mult)
                link(nc.vector.tensor_tensor(one2[:, h, :, :], one2[:, h, :, :], wide(top[:, h, 6, :]), ALU.mult))
                link(nc.vector.tensor_tensor(g[:, h, :, :], one1[:, h, :, :], one2[:, h, :, :], ALU.add))
                link(nc.vector.tensor_copy(gs[:, h, :, 0:E], g[:, h, :, :]))
                nc.vector.tensor_tensor(gs[:, h, :, E:2 * E], g[:, h, :, :], f32(gs[:, h, :, 0:E]),
                                        ALU.subtract).then_inc(dve_gate, 1)

            move_t(0)
            move_xff(0)
            move_u(0)
            mask_and_expand(0)
            move_t(1)
            move_xff(1)
            move_u(1)
            dve.wait_ge(act_gw, 1)
            nc.vector.tensor_tensor(gw_lo[:, :], gw_raw[:, :], f32(gw_hi[:, :]), ALU.subtract).then_inc(dve_gw, 1)
            residual(0)
            mask_and_expand(1)
            second_norm(0)
            low_part(0)
            gates(0)
            residual(1)
            spread_gates(0)
            second_norm(1)
            low_part(1)

            def gated(k):
                h, p = STEPS[k]
                dve.wait_ge(pe_o, k + 1)
                dve.wait_ge(act_g, k + 1)
                if p == 0:
                    dst = acc[:, h, :]
                else:
                    dst = part[:, k % 2, :]
                    if p > 2:
                        dve.wait_ge(pool_acc, h * (EP - 2) + p - 2)
                    elif p > 0 and h:
                        dve.wait_ge(pe_fin, 1)
                nc.vector.scalar_tensor_tensor(out=dst, in0=bank[4 + k % 2][:, 0:N],
                                               scalar=b12T[:, E + p:E + p + 1], in1=gbc[:, k % 2, :],
                                               op0=ALU.add, op1=ALU.mult).then_inc(dve_part, 1)

            def finish_statistics(h):
                dve.wait_ge(pe_fin, h + 1)
                link(nc.vector.tensor_tensor(half(y2, h), bank[7][0:T, 0:TH * D].rearrange("p (t d) -> p t d", d=D),
                                             half(xn2, h), ALU.add))
                statistics(3, y2, h)

            def finish(h):
                link(normalise(3, y2, y2, h))
                link(nc.vector.tensor_tensor(half(y2, h), half(y2, h), bcast(ffng), ALU.mult))
                dve.wait_ge(pool_h1b, h + 1)
                nc.vector.tensor_tensor(half(res, h), half(y2, h), half(h1b, h), ALU.add).then_inc(dve_out, 1)

            for k, (h, p) in enumerate(STEPS):
                dve.wait_ge(pe_z, 2 * k + 2)
                if k >= 2:
                    dve.wait_ge(pe_o, k - 1)
                nc.vector.tensor_scalar(h1e[:, k % 2, 1, :], bank[2 * (k % 2) + 1][:, 0:N],
                                        b12T[:, 2 * p + 1:2 * p + 2], 0.0, ALU.add, ALU.max).then_inc(dve_z, 1)
                if k:
                    gated(k - 1)
                if k == 2:
                    gates(1)
                if k == 4:
                    spread_gates(1)
                if k == EP + 1:
                    finish_statistics(0)
                if k == EP + 4:
                    finish(0)
            gated(len(STEPS) - 1)
            finish_statistics(1)
            finish(1)

        @block.tensor
        def _(pe):
            mm = nc.tensor.matmul
            pe.wait_ge(ld_c, 16)
            pe.wait_ge(ld_tokw, 16)
            for c in range(2):
                last = nc.tensor.transpose(bank[3][:, c * D:(c + 1) * D], w_raw[:, c * C:(c + 1) * C], ident[0:D, 0:D])
            last.then_inc(pe_tokwT, 1)
            for i, (q0, q1) in enumerate(((0, 8), (8, Q))):
                pe.wait_ge(ld_x[i], 16)
                for q in range(q0, q1):
                    last = nc.tensor.transpose(bank[i][:, (q - q0) * B:(q - q0 + 1) * B], xb[:, q * C:(q + 1) * C],
                                               ident[0:B, 0:B])
                last.then_inc(pe_xT, 1)
            pe.wait_ge(dve_wh, 1)
            pe.wait_ge(ld_b12, 32)
            for p in range(HP):
                nc.tensor.transpose(bank[5][:, p * D:(p + 1) * D],
                                    wk_h[:, 2 * p:2 * p + 2, :],
                                    ident[0:D, 0:D])
            nc.tensor.transpose(bank[5][:, HP * D:HP * D + E + EP], b12_raw[:, :],
                                ident[0:E + EP, 0:E + EP]).then_inc(pe_wkT, 1)
            pe.wait_ge(act_wh, 1)
            for p in range(HP):
                last = nc.tensor.transpose(bank[4][:, p * 128:(p + 1) * 128],
                                           wq_h[:, 2 * p:2 * p + 2, :],
                                           ident)
            last.then_inc(pe_wqT, 1)
            pe.wait_ge(act_wh, 2)
            for p in range(HP):
                last = nc.tensor.transpose(bank[6][:, p * 128:(p + 1) * 128],
                                           wv_h[:, 2 * p:2 * p + 2, :],
                                           ident)
            last.then_inc(pe_wvT, 1)
            pe.wait_ge(act_tokwT, 1)
            pe.wait_ge(act_xT, 1)
            pe.wait_ge(dve_xT, 1)
            for h in range(HALVES):
                for i, t in enumerate(tiles(h)):
                    for c in range(2):
                        last = mm(bank[2 + h][0:T, i * D:(i + 1) * D], xT[:, c, t * BT:(t + 1) * BT, :],
                                  tokwT[:, c, :], start=(c == 0), stop=(c == 1))
                last.then_inc(pe_y, 1)
            pe.wait_ge(act_wkT, 1)
            pe.wait_ge(act_wqT, 1)
            for par, bk in enumerate((7, 0)):
                r = slice(par * D, (par + 1) * D)
                for p in range(HP):
                    last = mm(bank[bk][:, p * D:(p + 1) * D], wqT[r, p, :], wkT[r, p, :], start=True, stop=True)
                last.then_inc(pe_a, 1)
            pe.wait_ge(act_wvT, 1)
            for par, bk in enumerate((1, 6)):
                r = slice(par * D, (par + 1) * D)
                for p in range(HP):
                    last = mm(bank[bk][:, p * D:(p + 1) * D], wvT[r, p, :], wo_sb[r, p, :], start=True, stop=True)
                last.then_inc(pe_b, 1)

            def features_first(h):
                pe.wait_ge(dve_lo, h + 1)
                for i, t in enumerate(tiles(h)):
                    last = nc.tensor.transpose(bank[2][:, i * T:(i + 1) * T], f32(stack[:, t, :, :]),
                                               ident[0:T, 0:T])
                last.then_inc(pe_xs, 1)

            def rejoin(h):
                mm(bank[4][:, :], fold[:, :, :], xs[:, h * TH * QUADS:(h + 1) * TH * QUADS, :],
                   start=True, stop=True).then_inc(pe_xff, 1)

            def queries(h, p, bk):
                rhs = xs[:, h * TH * QUADS:(h + 1) * TH * QUADS, 0:W]
                mm(bank[bk][:, 0:N], a_hi[:, p, :, :], rhs, start=True, stop=False)
                mm(bank[bk][:, 0:N], a_lo[:, p, :, :], rhs, start=False, stop=True).then_inc(pe_t, 1)

            def values(t, bk):
                lhs = xs[:, t * QUADS:(t + 1) * QUADS, :]
                mm(bank[bk][:, :], lhs, b_hi[:, :, :, :], start=True, stop=False)
                mm(bank[bk][:, :], lhs, b_lo[:, :, :, :], start=False, stop=True).then_inc(pe_u, 1)

            def scores(h, bk):
                for par in range(2):
                    r = slice(par * D, (par + 1) * D)
                    for i, t in enumerate(tiles(h)):
                        for q in range(QUADS):
                            at = t * T + q * W
                            last = mm(bank[bk[par]][q * PAD:(q + 1) * PAD, i * HP * W:(i + 1) * HP * W],
                                      xff[r, t * QUADS + q, :], tT[r, :, at:at + W], start=True, stop=True,
                                      tile_position=(par * D, q * PAD))
                    last.then_inc(pe_s, 1)

            def attend(h):
                pe.wait_ge(act_bd, 2 * h + 2)
                pe.wait_ge(dve_bd, 2 * h + 2)
                for tp in range(TH // 2):
                    for hd in range(H):
                        for i in range(2):
                            t = 2 * tp + i
                            row = ((hd % 2) * TH + t) * HP + hd // 2
                            last = mm(bank[h][i * D:(i + 1) * D, tp * T:(tp + 1) * T],
                                      u[:, h * TH + t, hd * D:(hd + 1) * D],
                                      bd[:, h, row, :, :], start=(hd == 0), stop=(hd == H - 1))
                last.then_inc(pe_av, 1)

            def tokens_first(h, bk):
                pe.wait_ge(act_oT, h + 1)
                for tp in range(TH // 2):
                    last = nc.tensor.transpose(bank[bk][0:T, tp * 128:(tp + 1) * 128],
                                               oT[:, h, tp * T:(tp + 1) * T], ident)
                last.then_inc(pe_oT, 1)

            def features_first2(h, bk):
                pe.wait_ge(dve_lo2, h + 1)
                for i, t in enumerate(tiles(h)):
                    last = nc.tensor.transpose(bank[bk][:, i * T:(i + 1) * T], f32(stack2[:, t, :, :]),
                                               ident[0:T, 0:T])
                last.then_inc(pe_xs2, 1)

            def gate_logits(h, bk):
                pe.wait_ge(act_xs2, h + 1)
                for i, t in enumerate(tiles(h)):
                    for w, first in ((gw_hi, True), (gw_lo, False)):
                        last = mm(bank[bk][0:T, i * E:(i + 1) * E], xs2[:, t * T:(t + 1) * T], w[:, :],
                                  start=first, stop=not first)
                last.then_inc(pe_lg, 1)

            pe.wait_ge(dve_y, 2)
            features_first(0)
            pe.wait_ge(dve_a, 2)
            pe.wait_ge(dve_b, 2)
            pe.wait_ge(act_xs, 1)
            for p, bk in enumerate((0, 1, 6, 7)):
                queries(0, p, bk)
            pe.wait_ge(dve_fold, 1)
            rejoin(0)
            pe.wait_ge(dve_xff, 1)
            for i, bk in enumerate((2, 3, 4, 5)):
                values(i, bk)
            pe.wait_ge(act_u, 2)
            features_first(1)
            pe.wait_ge(act_t, 2)
            pe.wait_ge(dve_t, 2)
            scores(0, (0, 1))
            pe.wait_ge(dve_u, 2)
            pe.wait_ge(act_xs, 2)
            for p, bk in enumerate((6, 7, 3, 5)):
                queries(1, p, bk)
            rejoin(1)
            attend(0)
            pe.wait_ge(dve_xff, 2)
            pe.wait_ge(act_t, 3)
            pe.wait_ge(dve_t, 3)
            for i, bk in enumerate((2, 4, 6, 7)):
                values(TH + i, bk)
            pe.wait_ge(act_t, 4)
            pe.wait_ge(dve_t, 4)
            scores(1, (1, 3))
            tokens_first(0, 5)
            pe.wait_ge(act_u, 4)
            pe.wait_ge(dve_u, 4)
            attend(1)
            features_first2(0, 0)
            pe.wait_ge(dve_gw, 1)
            gate_logits(0, 2)
            tokens_first(1, 3)

            def layer1(k):
                h, p = STEPS[k]
                if k >= 2:
                    pe.wait_ge(act_z, k - 1)
                    pe.wait_ge(dve_z, k - 1)
                for i in range(2):
                    z = bank[2 * (k % 2) + i][:, 0:N]
                    rhs = xs2[:, h * N:(h + 1) * N]
                    mm(z, w1_hi[:, 2 * p + i, :], rhs, start=True, stop=False)
                    mm(z, w1_lo[:, 2 * p + i, :], rhs, start=False, stop=True).then_inc(pe_z, 1)

            def spread(k):
                h, p = STEPS[k]
                pe.wait_ge(act_gT, h + 1)
                if k:
                    pe.wait_ge(act_g, k)
                mm(bank[6][:, 0:N], sel[:, p * 128:(p + 1) * 128], gT[:, h * N:(h + 1) * N],
                   start=True, stop=True).then_inc(pe_g, 1)

            def layer2(k):
                h, p = STEPS[k]
                pe.wait_ge(act_z, k + 1)
                pe.wait_ge(dve_z, k + 1)
                if k >= 2:
                    pe.wait_ge(dve_part, k - 1)
                for i in range(2):
                    last = mm(bank[4 + k % 2][i * D:(i + 1) * D, 0:N], w2_sb[:, 2 * p + i, :], h1e[:, k % 2, i, :],
                              start=True, stop=True)
                last.then_inc(pe_o, 1)

            def gates_first(h, bk):
                pe.wait_ge(dve_gate, h + 1)
                for i in range(TH):
                    last = nc.tensor.transpose(bank[bk][0:2 * E, i * T:(i + 1) * T], f32(gs[:, h, i, :]),
                                               ident[0:T, 0:T])
                last.then_inc(pe_gT, 1)

            def collect(h):
                pe.wait_ge(pool_acc, (h + 1) * (EP - 2))
                k = (h + 1) * EP - 1
                pe.wait_ge(dve_part, k + 1)
                for i in range(TH):
                    mm(bank[7][0:T, i * D:(i + 1) * D], acc[:, h, i * T:(i + 1) * T], idup, start=True, stop=False)
                    last = mm(bank[7][0:T, i * D:(i + 1) * D], part[:, k % 2, i * T:(i + 1) * T], idup,
                              start=False, stop=True)
                last.then_inc(pe_fin, 1)

            pe.wait_ge(pool_w1, 4)
            pe.wait_ge(act_oT, 2)
            layer1(0)
            pe.wait_ge(dve_h1, 1)
            features_first2(1, 5)
            gates_first(0, 4)
            pe.wait_ge(dve_h1, 2)
            layer1(1)
            gate_logits(1, 7)
            pe.wait_ge(act_sel, 1)
            pe.wait_ge(ld_w2, 16)
            spread(0)
            for k in range(len(STEPS)):
                if k:
                    if k > 1:
                        layer1(k)
                    if k == EP - 1:
                        gates_first(1, 7)
                    spread(k)
                    layer2(k - 1)
                if k == EP:
                    pe.wait_ge(act_gT, 2)
                    collect(0)
            layer2(len(STEPS) - 1)
            pe.wait_ge(dve_var, 7)
            collect(1)


_INS = ['x', 'L0_tok_W', 'L0_tok_b', 'L0_tok_gamma', 'L0_tok_beta', 'L0_attn_Wq', 'L0_attn_Wk', 'L0_attn_Wv',
        'L0_attn_Wo', 'L0_ffn_gate_w', 'L0_ffn_gate_b', 'L0_ffn_w1', 'L0_ffn_b1', 'L0_ffn_w2', 'L0_ffn_b2',
        'L0_ffn_gamma', 'L0_ffn_beta']


def kernel(**inputs):
    import numpy as _np
    import concourse.bacc as _bacc
    from concourse import mybir as _mybir
    from concourse.bass_utils import run_bass_kernel_spmd as _run

    row = _np.arange(128)[:, None]
    r = row % PAD
    i = _np.arange(W)[None, :]
    c_main = _np.concatenate([
        _np.eye(128), row % D == _np.arange(D)[None, :], (r < W) & (r // P == i // P),
        _np.broadcast_to(E - _np.arange(E)[None, :], (128, E))], axis=1).astype(_np.float32)
    k = _np.arange(2 * E)[:, None, None] % E
    pair, col = _np.arange(EP)[None, :, None], _np.arange(128)[None, None, :]
    c_sel = (k == 2 * pair + col // D).astype(_np.float32).reshape(2 * E, EP * 128)

    nc = _bacc.Bacc("TRN2", target_bir_lowering=False, num_devices=1)
    arrays, args = {}, []
    for name, a in [(n, inputs[n]) for n in _INS] + [("c_main", c_main), ("c_sel", c_sel)]:
        a = _np.ascontiguousarray(a)
        arrays[f"in_{name}_dram"] = a
        args.append(nc.dram_tensor(f"in_{name}_dram", a.shape, _mybir.dt.from_np(a.dtype), kind="ExternalInput").ap())
    out = nc.dram_tensor("out_dram", (B, P, D), _mybir.dt.float32, kind="ExternalOutput").ap()
    audio_tower(nc, *args, out)
    res = _run(nc, [arrays], core_ids=[0])
    return res.results[0]["out_dram"]
```

```python
from contextlib import ExitStack

import concourse.bass as bass
from concourse import mybir

B, S, FEAT = 64, 125, 16
PATCH, STRIDE = 16, 8
P = (S - PATCH) // STRIDE + 1
D, H, E, F = 64, 8, 16, 128
C = STRIDE * FEAT
Q = P + PATCH // STRIDE - 1
TOK = B * P
T = 112
NT = TOK // T
BT = T // P
HALVES = 2
TH = NT // HALVES
N = TH * T
QUADS = 4
W = T // QUADS
PAD = 32
HP = H // 2
EP = E // 2
EPS = 1e-5
APART = -2.0 ** 100
ROWS = 6 * D + 2 * E + E + EP


def audio_tower(nc, x_in, first_in, rows_in, qk_in, vo_in, w1_in, w2_in, gate_in, sel_in, out):
    F32, F32R = mybir.dt.float32, mybir.dt.float32r
    ALU, ACT, AX = mybir.AluOpType, mybir.ActivationFunctionType, mybir.AxisListType

    ctx = ExitStack()
    with ctx:
        def sb(name, shape, dt=F32):
            return ctx.enter_context(nc.sbuf_tensor(name, shape, dt))

        def sem(name):
            return ctx.enter_context(nc.semaphore(name))

        def f32(ap):
            return ap.bitcast(F32)

        first = sb("first", [128, 2 * D + 128])
        tokwT = first[:, 0:2 * D].rearrange("p (c d) -> p c d", d=D)
        ident = first[:, 2 * D:2 * D + 128]
        rows = sb("rows", [128, ROWS])
        tokb, tokg, tokbe, ffng, ffnbe = (rows[0:T, i * D:(i + 1) * D] for i in range(5))
        gateb, ids = rows[0:T, 5 * D:5 * D + E], rows[0:T, 5 * D + E:5 * D + 2 * E]
        idup, b12T = rows[:, 5 * D + 2 * E:6 * D + 2 * E], rows[:, 6 * D + 2 * E:]
        qk_w = sb("qk_w", [128, 2, HP, 128])
        vo_w = sb("vo_w", [128, 2, HP, 128])
        gw_raw = sb("gw_raw", [128, E])
        w1_raw = sb("w1_raw", [128, E, F])
        w2_sb = sb("w2_sb", [128, E, D])
        sel_raw = sb("sel_raw", [2 * E, EP * 128 + 128 + N])
        sel = sb("sel", [2 * E, EP * 128], F32R)
        apart_j, apart_i = sb("apart_j", [2, 128], F32R), sb("apart_i", [2, N], F32R)
        fold = sb("fold", [128, 2, D], F32R)
        a_hi, a_lo = sb("a_hi", [128, HP, 2, D], F32R), sb("a_lo", [128, HP, 2, D], F32R)
        b_hi, b_lo = sb("b_hi", [128, HP, 2, D], F32R), sb("b_lo", [128, HP, 2, D], F32R)
        gw_hi, gw_lo = sb("gw_hi", [128, E], F32R), sb("gw_lo", [128, E], F32R)
        w1_hi, w1_lo = sb("w1_hi", [128, E, F], F32R), sb("w1_lo", [128, E, F], F32R)
        xT = sb("xT", [128, HALVES, 2, N])
        warm = sb("warm", [128, 1])
        idle = sb("idle", [128, 512], mybir.dt.bfloat16)
        yb = sb("yb", [T, NT, D])
        h0 = sb("h0", [T, NT, D])
        h1 = sb("h1", [T, NT, D])
        xn = sb("xn", [T, NT, D])
        dev = sb("dev", [T, NT, D])
        xn2 = sb("xn2", [T, NT, D])
        y2 = sb("y2", [T, NT, D])
        h1b = sb("h1b", [T, NT, D])
        res = sb("res", [T, NT, D])
        stack = sb("stack", [T, NT, 2, D], F32R)
        stack2 = sb("stack2", [T, NT, 2, D], F32R)
        stats = sb("stats", [T, 4, NT, 6])
        mv = sb("mv", [T, 4, NT, 2])
        var = sb("var", [T, 4, NT])
        rstd = sb("rstd", [T, 4, NT])
        mhalf = sb("mhalf", [T, NT])
        xs = sb("xs", [128, NT * QUADS, PAD], F32R)
        xff = sb("xff", [128, NT * QUADS, PAD])
        tT = sb("tT", [128, HP, TOK])
        u = sb("u", [128, NT, H * D])
        att = sb("att", [128, HALVES, TH // 2, 4 * HP, W])
        bd = sb("bd", [128, HALVES, TH // 2, 4 * HP, QUADS, W])
        oT = sb("oT", [128, HALVES, TH // 2 * T])
        xs2 = sb("xs2", [128, TOK], F32R)
        lg = sb("lg", [T, HALVES, TH, E])
        one1 = sb("one1", [T, HALVES, TH, E])
        one2 = sb("one2", [T, HALVES, TH, E])
        g = sb("g", [T, HALVES, TH, E])
        top8 = sb("top8", [T, HALVES, TH, 8])
        at8 = sb("at8", [T, HALVES, TH, 8], mybir.dt.uint32)
        gap = sb("gap", [T, HALVES, 3, TH])
        gs = sb("gs", [T, HALVES, TH, 2 * E], F32R)
        gT = sb("gT", [2 * E, TOK], F32R)
        h1e = sb("h1e", [128, 2, 2, N])
        gbc = sb("gbc", [128, 2, N])
        xT_flat = xT[:, :, :, :].rearrange("c h k n -> c (h k n)")
        part = xT_flat[:, 0:2 * N].rearrange("p (i n) -> p i n", n=N)
        acc = xT_flat[:, 2 * N:4 * N].rearrange("p (i n) -> p i n", n=N)

        bank = [ctx.enter_context(nc.psum_tensor(f"bank{i}", [128, 512], F32)) for i in range(8)]

        ld_x = [sem(f"ld_x{i}") for i in range(HALVES)]
        ld_first, ld_rows, ld_qk, ld_vo, ld_gw, ld_w1, ld_w2, ld_sel = (
            sem(n) for n in ("ld_first", "ld_rows", "ld_qk", "ld_vo", "ld_gw", "ld_w1", "ld_w2", "ld_sel"))
        stored = sem("stored")
        (pe_y, pe_a, pe_b, pe_xs, pe_xff, pe_t, pe_u, pe_s, pe_av, pe_oT, pe_xs2, pe_lg, pe_gT, pe_z, pe_g, pe_o,
         pe_fin) = (sem(n) for n in (
             "pe_y", "pe_a", "pe_b", "pe_xs", "pe_xff", "pe_t", "pe_u", "pe_s", "pe_av", "pe_oT", "pe_xs2", "pe_lg",
             "pe_gT", "pe_z", "pe_g", "pe_o", "pe_fin"))
        (act_a, act_b, act_w1, act_hi, act_xs, act_t, act_u, act_sig, act_bd, act_oT, act_hi2, act_xs2, act_top,
         act_gT, act_z, act_g, act_sel, act_gw) = (sem(n) for n in (
             "act_a", "act_b", "act_w1", "act_hi", "act_xs", "act_t", "act_u", "act_sig", "act_bd", "act_oT",
             "act_hi2", "act_xs2", "act_top", "act_gT", "act_z", "act_g", "act_sel", "act_gw"))
        (dve_link, dve_idle, dve_zero, dve_y, dve_var, dve_xn, dve_lo, dve_a, dve_b, dve_xff, dve_t, dve_u, dve_bd,
         dve_h1, dve_xn2, dve_lo2, dve_lg, dve_gap, dve_gate, dve_z, dve_part, dve_out, dve_gw, dve_fold) = (
             sem(n) for n in (
                 "dve_link", "dve_idle", "dve_zero", "dve_y", "dve_var", "dve_xn", "dve_lo", "dve_a", "dve_b",
                 "dve_xff", "dve_t", "dve_u", "dve_bd", "dve_h1", "dve_xn2", "dve_lo2", "dve_lg", "dve_gap",
                 "dve_gate", "dve_z", "dve_part", "dve_out", "dve_gw", "dve_fold"))
        pool_pads, pool_bd, pool_half, pool_rstd, pool_w1, pool_acc, pool_h1b = (
            sem(n) for n in ("pool_pads", "pool_bd", "pool_half", "pool_rstd", "pool_w1", "pool_acc", "pool_h1b"))

        block = ctx.enter_context(nc.Block())

        def tiles(h):
            return range(h * TH, (h + 1) * TH)

        def half(ap, h):
            return ap[:, h * TH:(h + 1) * TH, :]

        NORMS = [(0, 0), (1, 0), (0, 1), (1, 1), (2, 0), (2, 1), (3, 0), (3, 1)]
        STEPS = [(h, p) for h in range(HALVES) for p in range(EP)]

        @block.sync
        def _(sp):
            sp.dma_start(xT[:, 0, :, :], x_in[0]).then_inc(ld_x[0], 16)
            sp.dma_start(qk_w[:, :, :, :], qk_in).then_inc(ld_qk, 16)
            sp.dma_start(xT[:, 1, :, :], x_in[1]).then_inc(ld_x[1], 16)
            sp.dma_start(vo_w[:, :, :, :], vo_in).then_inc(ld_vo, 16)
            sp.dma_start(w1_raw[:, :, :], w1_in).then_inc(ld_w1, 16)
            sp.dma_start(w2_sb[:, :, :], w2_in).then_inc(ld_w2, 16)
            ov = out.rearrange("b p d -> (b p) d").rearrange("(t p) d -> p t d", p=T)
            for h in range(HALVES):
                sp.wait_ge(dve_out, h + 1)
                sp.dma_start(ov[:, h * TH:(h + 1) * TH, :], half(res, h)).then_inc(stored, 16)
            sp.wait_ge(stored, 16 * HALVES)

        @block.gpsimd
        def _(pool):
            nc.gpsimd.memset(mhalf[:, :], -0.5).then_inc(pool_half, 1)
            nc.gpsimd.memset(f32(xs[:, :, :]), 0.0).then_inc(pool_pads, 1)
            nc.gpsimd.memset(bd[:, 0, :, :, :, :], 0.0).then_inc(pool_bd, 1)

            def inverse_root(n, h):
                pool.wait_ge(dve_var, NORMS.index((n, h)) + 1)
                nc.gpsimd.tensor_tensor(rstd[:, n, h * TH:(h + 1) * TH], var[:, n, h * TH:(h + 1) * TH],
                                        mhalf[:, h * TH:(h + 1) * TH], ALU.pow).then_inc(pool_rstd, 1)

            pool.wait_ge(pool_half, 1)
            w1_chunks = iter(range(8))

            def w1_low(n):
                for _, c in zip(range(n), w1_chunks):
                    r = slice(c * E // 8, (c + 1) * E // 8)
                    nc.gpsimd.tensor_tensor(w1_lo[:, r, :], w1_raw[:, r, :], f32(w1_hi[:, r, :]),
                                            ALU.subtract).then_inc(pool_w1, 1)

            inverse_root(0, 0)
            inverse_root(1, 0)
            pool.wait_ge(act_w1, 1)
            w1_low(1)
            inverse_root(0, 1)
            w1_low(1)
            inverse_root(1, 1)
            w1_low(6)
            inverse_root(2, 0)
            inverse_root(2, 1)
            for h in range(HALVES):
                pool.wait_ge(dve_h1, h + 1)
                nc.gpsimd.tensor_tensor(half(h1b, h), half(h1, h), ffnbe.unsqueeze(1).broadcast_to([T, TH, D]),
                                        ALU.add).then_inc(pool_h1b, 1)
            for k, (h, p) in enumerate(STEPS):
                if 0 < p < EP - 1:
                    pool.wait_ge(dve_part, k + 1)
                    if p > 1:
                        pool.wait_ge(pool_acc, h * (EP - 2) + p - 1)
                    nc.gpsimd.tensor_tensor(acc[:, h, :], acc[:, h, :], part[:, k % 2, :],
                                            ALU.add).then_inc(pool_acc, 1)
                if h == 1 and p == 2:
                    inverse_root(3, 0)
            inverse_root(3, 1)

        @block.scalar
        def _(act):
            act.dma_start(first[:, :], first_in).then_inc(ld_first, 16)
            act.dma_start(rows[:, :], rows_in).then_inc(ld_rows, 16)
            act.dma_start(gw_raw[:, :], gate_in).then_inc(ld_gw, 16)
            act.dma_start(sel_raw[:, :], sel_in).then_inc(ld_sel, 16)
            act.wait_ge(dve_idle, 1)
            nc.scalar.activation(warm[:, :], idle[:, 0:1], ACT.Sigmoid)
            def folded_high(dst, bk, ready, signal):
                act.wait_ge(ready, 1)
                nc.scalar.copy(dst[:, :, :, :], bank[bk][:, :]).then_inc(signal, 1)

            folded_high(a_hi, 7, pe_a, act_a)
            act.wait_ge(ld_w1, 16)
            nc.scalar.copy(w1_hi[:, :, :], w1_raw[:, :, :]).then_inc(act_w1, 1)
            folded_high(b_hi, 6, pe_b, act_b)
            act.wait_ge(ld_gw, 16)
            nc.scalar.copy(gw_hi[:, :], gw_raw[:, :]).then_inc(act_gw, 1)
            def high_part(dst, src, ready, signal, h):
                act.wait_ge(ready, h + 1)
                nc.scalar.copy(dst[:, h * TH:(h + 1) * TH, 0, :], half(src, h)).then_inc(signal, 1)

            high_part(stack, xn, dve_xn, act_hi, 0)
            act.wait_ge(ld_sel, 16)
            nc.scalar.copy(apart_j[:, :], sel_raw[0:2, EP * 128:EP * 128 + 128])
            nc.scalar.copy(apart_i[:, :], sel_raw[0:2, EP * 128 + 128:]).then_inc(act_sel, 1)

            T_BANK = ((0, 1, 7, 6), (6, 7, 3, 5))
            U_BANK = ((2, 3, 5, 4), (2, 4, 6, 7))
            S_BANK = ((0, 1), (1, 3))

            def move_xs(h):
                act.wait_ge(pool_pads, 1)
                act.wait_ge(pe_xs, h + 1)
                nc.scalar.copy(xs[:, h * TH * QUADS:(h + 1) * TH * QUADS, 0:W],
                               bank[2][:, 0:N].rearrange("p (q w) -> p q w", w=W)).then_inc(act_xs, 1)

            def move_t(h):
                for p in (0, 2):
                    act.wait_ge(pe_t, HP * h + p + 1)
                    nc.scalar.copy(tT[:, p, h * N:(h + 1) * N], bank[T_BANK[h][p]][:, 0:N]).then_inc(act_t, 1)

            def move_u(h):
                for i in (0, 2):
                    act.wait_ge(pe_u, TH * h + i + 1)
                    nc.scalar.copy(u[:, h * TH + i, :], bank[U_BANK[h][i]][:, :]).then_inc(act_u, 1)

            def sigmoids(h):
                for par in range(2):
                    act.wait_ge(pe_s, 2 * h + par + 1)
                    nc.scalar.activation(att[:, h, :, par * 2 * HP:(par + 1) * 2 * HP, :],
                                         bank[S_BANK[h][par]][:, 0:N].rearrange("p (c a w) -> p c a w", a=2 * HP, w=W),
                                         ACT.Sigmoid, scale=float(D) ** 0.5).then_inc(act_sig, 1)

            def expand(h):
                act.wait_ge(act_sig, 2 * h + 2)
                if h == 0:
                    act.wait_ge(pool_bd, 1)
                else:
                    act.wait_ge(dve_zero, 1)
                for tp in range(TH // 2):
                    for q in (0, 1):
                        r = slice(q * PAD, (q + 1) * PAD)
                        nc.scalar.copy(bd[r, h, tp, :, q, :], att[r, h, tp, :, :]).then_inc(act_bd, 1)

            def move_av(h):
                act.wait_ge(pe_av, h + 1)
                nc.scalar.activation(oT[:, h, :], bank[h][:, 0:TH // 2 * T], ACT.Relu).then_inc(act_oT, 1)

            def move_xs2(h):
                act.wait_ge(pe_xs2, h + 1)
                nc.scalar.copy(xs2[:, h * N:(h + 1) * N], bank[(0, 7)[h]][:, 0:N]).then_inc(act_xs2, 1)

            def gate_weights(h):
                act.wait_ge(dve_gap, h + 1)
                nc.scalar.activation(gap[:, h, 1, :], gap[:, h, 0, :], ACT.Sigmoid, scale=-1.0)
                nc.scalar.activation(gap[:, h, 2, :], gap[:, h, 0, :], ACT.Sigmoid).then_inc(act_top, 1)

            move_xs(0)
            move_t(0)
            move_u(0)
            high_part(stack, xn, dve_xn, act_hi, 1)
            move_xs(1)
            sigmoids(0)
            expand(0)
            move_t(1)
            move_av(0)
            move_u(1)
            sigmoids(1)
            expand(1)
            def move_gT(h):
                act.wait_ge(pe_gT, h + 1)
                nc.scalar.copy(gT[:, h * N:(h + 1) * N], bank[(6, 7)[h]][0:2 * E, 0:N]).then_inc(act_gT, 1)

            def hidden(k):
                h, p = STEPS[k]
                act.wait_ge(pe_z, 2 * k + 1)
                if k >= 2:
                    act.wait_ge(pe_o, k - 1)
                nc.scalar.activation(h1e[:, k % 2, 0, :], bank[2 * (k % 2)][:, 0:N], ACT.Relu,
                                     bias=b12T[:, 2 * p:2 * p + 1]).then_inc(act_z, 1)

            def move_gates(k):
                act.wait_ge(pe_g, k + 1)
                if k >= 2:
                    act.wait_ge(dve_part, k - 1)
                nc.scalar.copy(gbc[:, k % 2, :], bank[6][:, 0:N]).then_inc(act_g, 1)

            high_part(stack2, xn2, dve_xn2, act_hi2, 0)
            move_av(1)
            move_xs2(0)
            nc.scalar.copy(sel[:, :], sel_raw[:, 0:EP * 128]).then_inc(act_sel, 1)
            hidden(0)
            gate_weights(0)
            hidden(1)
            move_gT(0)
            move_gates(0)
            high_part(stack2, xn2, dve_xn2, act_hi2, 1)
            hidden(2)
            move_gates(1)
            move_xs2(1)
            for k in range(3, len(STEPS)):
                hidden(k)
                move_gates(k - 1)
                if k == 5:
                    gate_weights(1)
                if k == EP - 1:
                    move_gT(1)
            move_gates(len(STEPS) - 1)

        @block.vector
        def _(dve):
            made = [0]

            def link(ins):
                made[0] += 1
                ins.then_inc(dve_link, 1)
                dve.wait_ge(dve_link, made[0])

            def bcast(row):
                return row.unsqueeze(1).broadcast_to([T, TH, row.shape[-1]])

            def wide(col, n):
                return col.unsqueeze(2).broadcast_to([T, TH, n])

            def statistics(n, src, h, gamma=None):
                for t in tiles(h):
                    last = nc.vector.bn_stats(stats[:, n, t, :], src[:, t, :])
                link(last)
                for t in tiles(h):
                    last = nc.vector.bn_aggr(mv[:, n, t, :], stats[:, n, t, :])
                link(last)
                nc.vector.tensor_scalar(var[:, n, h * TH:(h + 1) * TH], mv[:, n, h * TH:(h + 1) * TH, 1], EPS, None,
                                        ALU.add).then_inc(dve_var, 1)
                last = nc.vector.tensor_tensor(half(dev, h), half(src, h),
                                               wide(mv[:, n, h * TH:(h + 1) * TH, 0], D), ALU.subtract)
                if gamma is not None:
                    link(last)
                    last = nc.vector.tensor_tensor(half(dev, h), half(dev, h), bcast(gamma), ALU.mult)
                link(last)

            def normalise(n, dst, h):
                dve.wait_ge(pool_rstd, NORMS.index((n, h)) + 1)
                return nc.vector.tensor_tensor(half(dst, h), half(dev, h),
                                               wide(rstd[:, n, h * TH:(h + 1) * TH], D), ALU.mult)

            nc.vector.memset(idle[:, :].bitcast(mybir.dt.uint32), 0).then_inc(dve_idle, 1)
            nc.vector.memset(bd[:, 1, :, :, :, :], 0.0).then_inc(dve_zero, 1)
            dve.wait_ge(ld_rows, 16)
            nc.vector.tensor_copy(fold[:, :, :], idup.unsqueeze(1).broadcast_to([128, 2, D])).then_inc(dve_fold, 1)

            def embed(h):
                dve.wait_ge(pe_y, h + 1)
                nc.vector.tensor_tensor(half(yb, h), bank[2 + h][0:T, 0:TH * D].rearrange("p (t d) -> p t d", d=D),
                                        bcast(tokb), ALU.add).then_inc(dve_y, 1)
                dve.wait_ge(dve_y, h + 1)
                statistics(0, yb, h, gamma=tokg)

            def embed_norm(h):
                link(normalise(0, h0, h))
                link(nc.vector.tensor_tensor(half(h0, h), half(h0, h), bcast(tokbe), ALU.add))
                statistics(1, h0, h)

            def folded_low(lo, hi, bk, ready, signal):
                dve.wait_ge(ready, 1)
                nc.vector.tensor_tensor(lo[:, :, :, :], bank[bk][:, :], f32(hi[:, :, :, :]),
                                        ALU.subtract).then_inc(signal, 1)

            def low(dst, src, high, ready, signal, h):
                dve.wait_ge(high, h + 1)
                dve.wait_ge(ready, h + 1)
                nc.vector.tensor_tensor(dst[:, h * TH:(h + 1) * TH, 1, :], half(src, h),
                                        f32(dst[:, h * TH:(h + 1) * TH, 0, :]), ALU.subtract).then_inc(signal, 1)

            embed(0)
            embed_norm(0)
            folded_low(a_lo, a_hi, 7, act_a, dve_a)
            normalise(1, xn, 0).then_inc(dve_xn, 1)
            embed(1)
            low(stack, xn, act_hi, dve_xn, dve_lo, 0)
            folded_low(b_lo, b_hi, 6, act_b, dve_b)
            embed_norm(1)

            T_BANK = ((0, 1, 7, 6), (6, 7, 3, 5))
            U_BANK = ((2, 3, 5, 4), (2, 4, 6, 7))

            def move_xff(h):
                dve.wait_ge(pe_xff, h + 1)
                nc.vector.tensor_copy(xff[:, h * TH * QUADS:(h + 1) * TH * QUADS, :],
                                      bank[4][:, :]).then_inc(dve_xff, 1)

            def move_t(h):
                for p in (1, 3):
                    dve.wait_ge(pe_t, HP * h + p + 1)
                    nc.vector.tensor_copy(tT[:, p, h * N:(h + 1) * N], bank[T_BANK[h][p]][:, 0:N]).then_inc(dve_t, 1)

            def move_u(h):
                for i in (1, 3):
                    dve.wait_ge(pe_u, TH * h + i + 1)
                    nc.vector.tensor_copy(u[:, h * TH + i, :], bank[U_BANK[h][i]][:, :]).then_inc(dve_u, 1)

            def expand(h):
                dve.wait_ge(act_sig, 2 * h + 2)
                if h == 0:
                    dve.wait_ge(pool_bd, 1)
                for tp in range(TH // 2):
                    for q in (2, 3):
                        r = slice(q * PAD, (q + 1) * PAD)
                        nc.vector.tensor_copy(bd[r, h, tp, :, q, :], att[r, h, tp, :, :]).then_inc(dve_bd, 1)

            def residual(h):
                dve.wait_ge(pe_oT, h + 1)
                nc.vector.tensor_tensor(half(h1, h), bank[(5, 7)[h]][0:T, 0:TH * D].rearrange("p (t d) -> p t d", d=D),
                                        half(h0, h), ALU.add).then_inc(dve_h1, 1)
                dve.wait_ge(dve_h1, h + 1)
                statistics(2, h1, h)

            def second_norm(h):
                normalise(2, xn2, h).then_inc(dve_xn2, 1)

            def gates(h):
                dve.wait_ge(pe_lg, h + 1)
                nc.vector.tensor_tensor(lg[:, h, :, :], bank[(6, 7)[h]][0:T, 0:TH * E].rearrange(
                    "p (t e) -> p t e", e=E), bcast(gateb), ALU.add).then_inc(dve_lg, 1)
                dve.wait_ge(dve_lg, h + 1)
                for i in range(TH):
                    last = nc.vector.max(top8[:, h, i, :], lg[:, h, i, :])
                link(last)
                nc.vector.tensor_tensor(gap[:, h, 0, :], top8[:, h, :, 1], top8[:, h, :, 0],
                                        ALU.subtract).then_inc(dve_gap, 1)
                for i in range(TH):
                    last = nc.vector.max_index(at8[:, h, i, :], top8[:, h, i, :], lg[:, h, i, :])
                link(last)

            def spread_gates(h):
                nc.vector.tensor_tensor(one1[:, h, :, :], bcast(ids), wide(at8[:, h, :, 0], E), ALU.is_equal)
                link(nc.vector.tensor_tensor(one2[:, h, :, :], bcast(ids), wide(at8[:, h, :, 1], E), ALU.is_equal))
                dve.wait_ge(act_top, h + 1)
                nc.vector.tensor_tensor(one1[:, h, :, :], one1[:, h, :, :], wide(gap[:, h, 1, :], E), ALU.mult)
                link(nc.vector.tensor_tensor(one2[:, h, :, :], one2[:, h, :, :], wide(gap[:, h, 2, :], E), ALU.mult))
                link(nc.vector.tensor_tensor(g[:, h, :, :], one1[:, h, :, :], one2[:, h, :, :], ALU.add))
                link(nc.vector.tensor_copy(gs[:, h, :, 0:E], g[:, h, :, :]))
                nc.vector.tensor_tensor(gs[:, h, :, E:2 * E], g[:, h, :, :], f32(gs[:, h, :, 0:E]),
                                        ALU.subtract).then_inc(dve_gate, 1)

            def gated(k):
                h, p = STEPS[k]
                dve.wait_ge(pe_o, k + 1)
                dve.wait_ge(act_g, k + 1)
                if p == 0:
                    dst = acc[:, h, :]
                else:
                    dst = part[:, k % 2, :]
                    if p > 2:
                        dve.wait_ge(pool_acc, h * (EP - 2) + p - 2)
                    elif p > 0 and h:
                        dve.wait_ge(pe_fin, 1)
                nc.vector.scalar_tensor_tensor(out=dst, in0=bank[4 + k % 2][:, 0:N],
                                               scalar=b12T[:, E + p:E + p + 1], in1=gbc[:, k % 2, :],
                                               op0=ALU.add, op1=ALU.mult).then_inc(dve_part, 1)

            def hidden(k):
                h, p = STEPS[k]
                dve.wait_ge(pe_z, 2 * k + 2)
                if k >= 2:
                    dve.wait_ge(pe_o, k - 1)
                nc.vector.tensor_scalar(h1e[:, k % 2, 1, :], bank[2 * (k % 2) + 1][:, 0:N],
                                        b12T[:, 2 * p + 1:2 * p + 2], 0.0, ALU.add, ALU.max).then_inc(dve_z, 1)

            def finish_statistics(h):
                dve.wait_ge(pe_fin, h + 1)
                link(nc.vector.tensor_tensor(half(y2, h), bank[7][0:T, 0:TH * D].rearrange("p (t d) -> p t d", d=D),
                                             half(xn2, h), ALU.add))
                statistics(3, y2, h, gamma=ffng)

            def finish(h):
                link(normalise(3, y2, h))
                dve.wait_ge(pool_h1b, h + 1)
                nc.vector.tensor_tensor(half(res, h), half(y2, h), half(h1b, h), ALU.add).then_inc(dve_out, 1)

            move_t(0)
            move_xff(0)
            normalise(1, xn, 1).then_inc(dve_xn, 1)
            move_u(0)
            low(stack, xn, act_hi, dve_xn, dve_lo, 1)
            expand(0)
            move_t(1)
            move_xff(1)
            dve.wait_ge(act_gw, 1)
            nc.vector.tensor_tensor(gw_lo[:, :], gw_raw[:, :], f32(gw_hi[:, :]), ALU.subtract).then_inc(dve_gw, 1)
            move_u(1)
            residual(0)
            expand(1)
            second_norm(0)
            low(stack2, xn2, act_hi2, dve_xn2, dve_lo2, 0)
            gates(0)
            hidden(0)
            spread_gates(0)
            hidden(1)
            residual(1)
            gated(0)
            second_norm(1)
            hidden(2)
            low(stack2, xn2, act_hi2, dve_xn2, dve_lo2, 1)
            gated(1)
            for k in range(3, len(STEPS)):
                hidden(k)
                gated(k - 1)
                if k == 4:
                    gates(1)
                if k == 6:
                    spread_gates(1)
                if k == EP + 1:
                    finish_statistics(0)
                if k == EP + 4:
                    finish(0)
            gated(len(STEPS) - 1)
            finish_statistics(1)
            finish(1)

        @block.tensor
        def _(pe):
            mm = nc.tensor.matmul
            def keep_warm(n):
                for _ in range(n):
                    mm(bank[5][:, :], idle[:, 0:128], idle[:, :], start=True, stop=True)

            pe.wait_ge(dve_idle, 1)
            keep_warm(5)
            pe.wait_ge(ld_first, 16)

            def embed(h):
                pe.wait_ge(ld_x[h], 16)
                for i in range(TH):
                    for c in range(2):
                        last = mm(bank[2 + h][0:T, i * D:(i + 1) * D], xT[:, h, c, i * T:(i + 1) * T],
                                  tokwT[:, c, :], start=(c == 0), stop=(c == 1))
                last.then_inc(pe_y, 1)

            def fold_weights(w, bk, loaded, signal):
                pe.wait_ge(loaded, 16)
                for p in range(HP):
                    last = mm(bank[bk][:, p * 128:(p + 1) * 128], w[:, 0, p, :], w[:, 1, p, :], start=True, stop=True)
                last.then_inc(signal, 1)

            embed(0)
            fold_weights(qk_w, 7, ld_qk, pe_a)
            embed(1)
            fold_weights(vo_w, 6, ld_vo, pe_b)

            def features_first(h):
                pe.wait_ge(dve_lo, h + 1)
                for i, t in enumerate(tiles(h)):
                    last = nc.tensor.transpose(bank[2][:, i * T:(i + 1) * T], f32(stack[:, t, :, :]),
                                               ident[0:T, 0:T])
                last.then_inc(pe_xs, 1)

            def rejoin(h):
                mm(bank[4][:, :], fold[:, :, :], xs[:, h * TH * QUADS:(h + 1) * TH * QUADS, :],
                   start=True, stop=True).then_inc(pe_xff, 1)

            def queries(h, p, bk):
                rhs = xs[:, h * TH * QUADS:(h + 1) * TH * QUADS, 0:W]
                mm(bank[bk][:, 0:N], a_hi[:, p, :, :], rhs, start=True, stop=False)
                mm(bank[bk][:, 0:N], a_lo[:, p, :, :], rhs, start=False, stop=True).then_inc(pe_t, 1)

            def values(t, bk):
                lhs = xs[:, t * QUADS:(t + 1) * QUADS, :]
                mm(bank[bk][:, :], lhs, b_hi[:, :, :, :], start=True, stop=False)
                mm(bank[bk][:, :], lhs, b_lo[:, :, :, :], start=False, stop=True).then_inc(pe_u, 1)

            def scores(h, bk):
                for par in range(2):
                    r = slice(par * D, (par + 1) * D)
                    mm(bank[bk[par]][:, 0:N], apart_j[:, :], apart_i[:, :], start=True, stop=True)
                    for i, t in enumerate(tiles(h)):
                        for q in range(QUADS):
                            at = t * T + q * W
                            last = mm(bank[bk[par]][q * PAD:(q + 1) * PAD, i * HP * W:(i + 1) * HP * W],
                                      xff[r, t * QUADS + q, :], tT[r, :, at:at + W], start=False, stop=True,
                                      skip_group_check=True,
                                      tile_position=(par * D, q * PAD))
                    last.then_inc(pe_s, 1)

            def attend(h):
                for tp in range(TH // 2):
                    pe.wait_ge(act_bd, 2 * (2 * h + tp + 1))
                    pe.wait_ge(dve_bd, 2 * (2 * h + tp + 1))
                    for hd in range(H):
                        for i in range(2):
                            t = 2 * tp + i
                            row = ((hd % 2) * 2 + i) * HP + hd // 2
                            last = mm(bank[h][i * D:(i + 1) * D, tp * T:(tp + 1) * T],
                                      u[:, h * TH + t, hd * D:(hd + 1) * D],
                                      bd[:, h, tp, row, :, :], start=(hd == 0), stop=(hd == H - 1))
                last.then_inc(pe_av, 1)

            def tokens_first(h, bk):
                pe.wait_ge(act_oT, h + 1)
                for tp in range(TH // 2):
                    last = nc.tensor.transpose(bank[bk][0:T, tp * 128:(tp + 1) * 128],
                                               oT[:, h, tp * T:(tp + 1) * T], ident)
                last.then_inc(pe_oT, 1)

            def features_first2(h, bk):
                pe.wait_ge(dve_lo2, h + 1)
                for i, t in enumerate(tiles(h)):
                    last = nc.tensor.transpose(bank[bk][:, i * T:(i + 1) * T], f32(stack2[:, t, :, :]),
                                               ident[0:T, 0:T])
                last.then_inc(pe_xs2, 1)

            def gate_logits(h, bk):
                pe.wait_ge(act_xs2, h + 1)
                for i, t in enumerate(tiles(h)):
                    for w, first in ((gw_hi, True), (gw_lo, False)):
                        last = mm(bank[bk][0:T, i * E:(i + 1) * E], xs2[:, t * T:(t + 1) * T], w[:, :],
                                  start=first, stop=not first)
                last.then_inc(pe_lg, 1)

            keep_warm(4)
            pe.wait_ge(dve_y, 1)
            features_first(0)
            pe.wait_ge(dve_a, 1)
            pe.wait_ge(act_xs, 1)
            queries(0, 0, 0)
            queries(0, 1, 1)
            queries(0, 2, 7)
            pe.wait_ge(dve_fold, 1)
            rejoin(0)
            pe.wait_ge(dve_b, 1)
            queries(0, 3, 6)
            pe.wait_ge(dve_y, 2)
            for i, bk in ((0, 2), (1, 3), (2, 5)):
                values(i, bk)
            pe.wait_ge(dve_xff, 1)
            values(3, 4)
            pe.wait_ge(act_t, 2)
            pe.wait_ge(dve_t, 2)
            pe.wait_ge(act_sel, 1)
            scores(0, (0, 1))
            pe.wait_ge(act_u, 1)
            features_first(1)
            pe.wait_ge(act_u, 2)
            pe.wait_ge(dve_u, 2)
            pe.wait_ge(act_xs, 2)
            for p, bk in enumerate((6, 7, 3, 5)):
                queries(1, p, bk)
            rejoin(1)
            attend(0)
            pe.wait_ge(dve_xff, 2)
            pe.wait_ge(act_t, 3)
            pe.wait_ge(dve_t, 3)
            for i, bk in enumerate((2, 4, 6, 7)):
                values(TH + i, bk)
            pe.wait_ge(act_t, 4)
            pe.wait_ge(dve_t, 4)
            tokens_first(0, 5)
            scores(1, (1, 3))
            pe.wait_ge(act_u, 4)
            pe.wait_ge(dve_u, 4)
            attend(1)
            features_first2(0, 0)
            pe.wait_ge(dve_gw, 1)
            gate_logits(0, 6)

            def layer1(k):
                h, p = STEPS[k]
                if k >= 2:
                    pe.wait_ge(act_z, k - 1)
                    pe.wait_ge(dve_z, k - 1)
                for i in range(2):
                    z = bank[2 * (k % 2) + i][:, 0:N]
                    rhs = xs2[:, h * N:(h + 1) * N]
                    mm(z, w1_hi[:, 2 * p + i, :], rhs, start=True, stop=False)
                    mm(z, w1_lo[:, 2 * p + i, :], rhs, start=False, stop=True).then_inc(pe_z, 1)

            def spread(k):
                h, p = STEPS[k]
                pe.wait_ge(act_gT, h + 1)
                if k:
                    pe.wait_ge(act_g, k)
                mm(bank[6][:, 0:N], sel[:, p * 128:(p + 1) * 128], gT[:, h * N:(h + 1) * N],
                   start=True, stop=True).then_inc(pe_g, 1)

            def layer2(k):
                h, p = STEPS[k]
                pe.wait_ge(act_z, k + 1)
                pe.wait_ge(dve_z, k + 1)
                if k >= 2:
                    pe.wait_ge(dve_part, k - 1)
                for i in range(2):
                    last = mm(bank[4 + k % 2][i * D:(i + 1) * D, 0:N], w2_sb[:, 2 * p + i, :], h1e[:, k % 2, i, :],
                              start=True, stop=True)
                last.then_inc(pe_o, 1)

            def gates_first(h, bk):
                pe.wait_ge(dve_gate, h + 1)
                for i in range(TH):
                    last = nc.tensor.transpose(bank[bk][0:2 * E, i * T:(i + 1) * T], f32(gs[:, h, i, :]),
                                               ident[0:T, 0:T])
                last.then_inc(pe_gT, 1)

            def collect(h):
                pe.wait_ge(pool_acc, (h + 1) * (EP - 2))
                k = (h + 1) * EP - 1
                pe.wait_ge(dve_part, k + 1)
                for i in range(TH):
                    mm(bank[7][0:T, i * D:(i + 1) * D], acc[:, h, i * T:(i + 1) * T], idup, start=True, stop=False)
                    last = mm(bank[7][0:T, i * D:(i + 1) * D], part[:, k % 2, i * T:(i + 1) * T], idup,
                              start=False, stop=True)
                last.then_inc(pe_fin, 1)

            pe.wait_ge(pool_w1, 8)
            pe.wait_ge(act_oT, 2)
            layer1(0)
            tokens_first(1, 7)
            layer1(1)
            pe.wait_ge(ld_w2, 16)
            layer2(0)
            layer1(2)
            gates_first(0, 6)
            layer2(1)
            pe.wait_ge(act_sel, 2)
            spread(0)
            layer1(3)
            pe.wait_ge(dve_h1, 2)
            features_first2(1, 7)
            spread(1)
            layer2(2)
            gate_logits(1, 7)
            spread(2)
            for k in range(4, len(STEPS)):
                layer1(k)
                if k == EP - 1:
                    gates_first(1, 7)
                layer2(k - 1)
                spread(k - 1)
                if k == EP + 1:
                    pe.wait_ge(act_gT, 2)
                    collect(0)
            layer2(len(STEPS) - 1)
            spread(len(STEPS) - 1)
            pe.wait_ge(dve_var, NORMS.index((3, 0)) + 1)
            collect(1)


def kernel(**inputs):
    import numpy as _np
    import concourse.bacc as _bacc
    from concourse import mybir as _mybir
    from concourse.bass_utils import run_bass_kernel_spmd as _run

    v = {n.removeprefix("L0_"): _np.asarray(a) for n, a in inputs.items()}
    f4 = _np.float32

    def spread_rows(a, n=128):
        return _np.broadcast_to(a[None, :], (n, a.shape[0]))

    def by_pair(a):
        return a.reshape(-1, D, HP, 2).transpose(3, 1, 2, 0).reshape(128, HP, -1)

    rows = v["x"].reshape(B, S * FEAT)[:, :Q * C].reshape(B, Q, C)
    patches = _np.stack([rows[:, c:c + P] for c in range(2)])
    x_in = patches.reshape(2, HALVES, N, C).transpose(1, 3, 0, 2)
    first = _np.concatenate([v["tok_W"].reshape(D, 2, C).transpose(2, 1, 0).reshape(C, 2 * D),
                             _np.eye(128, dtype=f4)], axis=1)
    idup = _np.tile(_np.eye(D, dtype=f4), (2, 1))
    b2_pairs = v["ffn_b2"].reshape(EP, 2 * D).T
    rows_in = _np.concatenate(
        [spread_rows(v[n]) for n in ("tok_b", "tok_gamma", "tok_beta", "ffn_gamma", "ffn_beta", "ffn_gate_b")]
        + [spread_rows(_np.arange(E, dtype=f4)), idup, v["ffn_b1"].T, b2_pairs], axis=1)

    def block_diagonal(a):
        out = _np.zeros((2, D, HP, 2, D), f4)
        for par in range(2):
            out[par, :, :, par, :] = a.reshape(2, D, HP, D)[par]
        return out.reshape(128, HP, 128)

    wo = v["attn_Wo"].reshape(D, HP, 2, D).transpose(2, 0, 1, 3).reshape(128, HP, D)
    qk_in = _np.stack([_np.tile(by_pair(v["attn_Wq"]), (1, 1, 2)), block_diagonal(by_pair(v["attn_Wk"]))], axis=1)
    vo_in = _np.stack([_np.tile(by_pair(v["attn_Wv"]), (1, 1, 2)), block_diagonal(wo)], axis=1)
    w1_in = _np.tile(v["ffn_w1"].transpose(1, 0, 2), (2, 1, 1))
    w2_in = v["ffn_w2"].transpose(1, 0, 2)
    gate_in = _np.tile(v["ffn_gate_w"], (2, 1))
    sel_in = _np.zeros((2 * E, EP * 128 + 128 + N), f4)
    k = _np.arange(2 * E)[:, None, None] % E
    pair, col = _np.arange(EP)[None, :, None], _np.arange(128)[None, None, :]
    sel_in[:, :EP * 128] = (k == 2 * pair + col // D).reshape(2 * E, EP * 128)
    clip, j, i = _np.arange(2)[:, None], _np.arange(128)[None, :] % PAD, _np.arange(N)[None, :] % W
    sel_in[0:2, EP * 128:EP * 128 + 128] = (j // P == clip) & (j < W)
    sel_in[0:2, EP * 128 + 128:] = _np.where(i // P == clip, 0.0, APART)

    nc = _bacc.Bacc("TRN2", target_bir_lowering=False, num_devices=1)
    arrays, args = {}, []
    for name, a in (("x", x_in), ("first", first), ("rows", rows_in), ("qk", qk_in), ("vo", vo_in), ("w1", w1_in),
                    ("w2", w2_in), ("gate", gate_in), ("sel", sel_in)):
        a = _np.ascontiguousarray(a)
        arrays[f"in_{name}_dram"] = a
        args.append(nc.dram_tensor(f"in_{name}_dram", a.shape, _mybir.dt.from_np(a.dtype), kind="ExternalInput").ap())
    out = nc.dram_tensor("out_dram", (B, P, D), _mybir.dt.float32, kind="ExternalOutput").ap()
    audio_tower(nc, *args, out)
    res = _run(nc, [arrays], core_ids=[0])
    return res.results[0]["out_dram"]
```

```python
from contextlib import ExitStack

import concourse.bass as bass
from concourse import mybir

B, S, FEAT = 64, 125, 16
PATCH, STRIDE = 16, 8
P = (S - PATCH) // STRIDE + 1
D, H, E, F = 64, 8, 16, 128
C = STRIDE * FEAT
Q = P + PATCH // STRIDE - 1
TOK = B * P
T = 112
NT = TOK // T
BT = T // P
HALVES = 2
TH = NT // HALVES
N = TH * T
QUADS = 4
W = T // QUADS
PAD = 32
HP = H // 2
EP = E // 2
EPS = 1e-5
APART = -2.0 ** 100
ROWS = 5 * D + 2 * E + E + EP


def audio_tower(nc, x_in, first_in, rows_in, qk_in, vo_in, w1_in, w2_in, gate_in, sel_in, out):
    F32, F32R = mybir.dt.float32, mybir.dt.float32r
    ALU, ACT, AX = mybir.AluOpType, mybir.ActivationFunctionType, mybir.AxisListType

    ctx = ExitStack()
    with ctx:
        def sb(name, shape, dt=F32):
            return ctx.enter_context(nc.sbuf_tensor(name, shape, dt))

        def sem(name):
            return ctx.enter_context(nc.semaphore(name))

        def f32(ap):
            return ap.bitcast(F32)

        first = sb("first", [128, 2 * D + 128 + D])
        tokwT = first[:, 0:2 * D].rearrange("p (c d) -> p c d", d=D)
        ident = first[:, 2 * D:2 * D + 128]
        tokb = first[0:1, 2 * D + 128:].unsqueeze(1).broadcast_to([1, TH, D])
        rows = sb("rows", [128, ROWS])
        tokg, tokbe, ffng, ffnbe = (rows[0:T, i * D:(i + 1) * D] for i in range(4))
        gateb, ids = rows[0:T, 4 * D:4 * D + E], rows[0:T, 4 * D + E:4 * D + 2 * E]
        idup, b12T = rows[:, 4 * D + 2 * E:5 * D + 2 * E], rows[:, 5 * D + 2 * E:]
        qk_w = sb("qk_w", [128, 2, HP, 128])
        vo_w = sb("vo_w", [128, 2, HP, 128])
        gw_raw = sb("gw_raw", [128, E])
        w1_raw = sb("w1_raw", [128, E, F])
        w2_sb = sb("w2_sb", [128, E, D])
        sel_raw = sb("sel_raw", [2 * E, EP * 128 + 128 + N])
        sel = sb("sel", [2 * E, EP * 128], F32R)
        apart_j, apart_i = sb("apart_j", [2, 128], F32R), sb("apart_i", [2, N], F32R)
        fold = sb("fold", [128, 2, D], F32R)
        a_hi, a_lo = sb("a_hi", [128, HP, 2, D], F32R), sb("a_lo", [128, HP, 2, D], F32R)
        b_hi, b_lo = sb("b_hi", [128, HP, 2, D], F32R), sb("b_lo", [128, HP, 2, D], F32R)
        gw = sb("gw", [128, 2, E], F32R)
        w1_hi, w1_lo = sb("w1_hi", [128, E, F], F32R), sb("w1_lo", [128, E, F], F32R)
        xT = sb("xT", [128, HALVES, 2, N])
        warm = sb("warm", [128, 1])
        idle = sb("idle", [128, 128], mybir.dt.bfloat16)
        ones = sb("ones", [1, T])
        h0 = sb("h0", [T, NT, D])
        xn = sb("xn", [T, NT, D])
        dev = sb("dev", [T, NT, D])
        xn2 = sb("xn2", [T, NT, D])
        h1b = sb("h1b", [T, NT, D])
        res = sb("res", [T, NT, D])
        stack = sb("stack", [T, NT, 2, D], F32R)
        stack2 = sb("stack2", [T, NT, 2, D], F32R)
        stats = sb("stats", [T, 4, NT, 6])
        mv = sb("mv", [T, 4, NT, 2])
        var = sb("var", [T, 4, NT])
        rstd = sb("rstd", [T, 4, NT])
        mhalf = sb("mhalf", [T, NT])
        xs = sb("xs", [128, NT * QUADS, PAD], F32R)
        xff = sb("xff", [128, NT * QUADS, PAD])
        tT = sb("tT", [128, HP, TOK])
        u = sb("u", [128, NT, H * D])
        att = sb("att", [128, HALVES, TH // 2, 4 * HP, W])
        bd = sb("bd", [128, HALVES, TH // 2, 4 * HP, QUADS, W])
        oT = sb("oT", [128, HALVES, TH // 2 * T])
        xs2 = sb("xs2", [128, TOK], F32R)
        lg = sb("lg", [T, HALVES, TH, E])
        one1 = sb("one1", [T, HALVES, TH, E])
        one2 = sb("one2", [T, HALVES, TH, E])
        g = sb("g", [T, HALVES, TH, E])
        top8 = sb("top8", [T, HALVES, TH, 8])
        at8 = sb("at8", [T, HALVES, TH, 8], mybir.dt.uint32)
        gap = sb("gap", [T, HALVES, 3, TH])
        gs = sb("gs", [T, HALVES, TH, 2 * E], F32R)
        gT = sb("gT", [2 * E, TOK], F32R)
        h1e = sb("h1e", [128, 2, 2, N])
        gbc = sb("gbc", [128, 2, N])
        xT_flat = xT[:, :, :, :].rearrange("c h k n -> c (h k n)")
        part = xT_flat[:, 0:2 * N].rearrange("p (i n) -> p i n", n=N)
        acc = xT_flat[:, 2 * N:4 * N].rearrange("p (i n) -> p i n", n=N)

        bank = [ctx.enter_context(nc.psum_tensor(f"bank{i}", [128, 512], F32)) for i in range(8)]

        ld_x = [sem(f"ld_x{i}") for i in range(3)]
        ld_first, ld_rows, ld_qk, ld_vo, ld_gw, ld_w1, ld_w2, ld_sel = (
            sem(n) for n in ("ld_first", "ld_rows", "ld_qk", "ld_vo", "ld_gw", "ld_w1", "ld_w2", "ld_sel"))
        stored = sem("stored")
        (pe_y, pe_a, pe_b, pe_xs, pe_xff, pe_t, pe_u, pe_s, pe_av, pe_oT, pe_xs2, pe_lg, pe_gT, pe_z, pe_g, pe_o,
         pe_fin) = (sem(n) for n in (
             "pe_y", "pe_a", "pe_b", "pe_xs", "pe_xff", "pe_t", "pe_u", "pe_s", "pe_av", "pe_oT", "pe_xs2", "pe_lg",
             "pe_gT", "pe_z", "pe_g", "pe_o", "pe_fin"))
        (act_a, act_b, act_w1, act_hi, act_xs, act_t, act_u, act_sig, act_bd, act_oT, act_hi2, act_xs2, act_top,
         act_gT, act_z, act_g, act_sel, act_gw) = (sem(n) for n in (
             "act_a", "act_b", "act_w1", "act_hi", "act_xs", "act_t", "act_u", "act_sig", "act_bd", "act_oT",
             "act_hi2", "act_xs2", "act_top", "act_gT", "act_z", "act_g", "act_sel", "act_gw"))
        (dve_link, dve_ones, dve_zero, dve_y, dve_var, dve_xn, dve_lo, dve_a, pool_b, dve_xff, dve_t, dve_u, dve_bd,
         dve_xn2, dve_lo2, dve_lg, dve_gap, dve_gate, dve_z, dve_part, dve_out, dve_gw, dve_fold,
         dve_h0, dve_xs, dve_fin, dve_dev, dve_acc, dve_h1, dve_h1b) = (
             sem(n) for n in (
                 "dve_link", "dve_ones", "dve_zero", "dve_y", "dve_var", "dve_xn", "dve_lo", "dve_a", "pool_b",
                 "dve_xff", "dve_t", "dve_u", "dve_bd", "dve_xn2", "dve_lo2", "dve_lg", "dve_gap",
                 "dve_gate", "dve_z", "dve_part", "dve_out", "dve_gw", "dve_fold", "dve_h0", "dve_xs", "dve_fin",
                 "dve_dev", "dve_acc", "dve_h1", "dve_h1b"))
        pool_idle, pool_pads, pool_bd, pool_half, pool_rstd, pool_w1, pool_acc = (
            sem(n) for n in ("pool_idle", "pool_pads", "pool_bd", "pool_half", "pool_rstd", "pool_w1", "pool_acc"))

        block = ctx.enter_context(nc.Block())

        def tiles(h):
            return range(h * TH, (h + 1) * TH)

        def span(ap, ts):
            return ap[:, ts[0]:ts[-1] + 1, :]

        def half(ap, h):
            return span(ap, tiles(h))

        PAIRS = [[range(h * TH, h * TH + TH // 2), range(h * TH + TH // 2, (h + 1) * TH)] for h in range(HALVES)]
        NORMS = [(0, PAIRS[0][0]), (0, PAIRS[0][1]), (1, PAIRS[0][0]), (1, PAIRS[0][1]), (0, tiles(1)), (1, tiles(1)),
                 (2, PAIRS[0][0]), (2, PAIRS[0][1]), (2, tiles(1)),
                 (3, tiles(0)), (3, PAIRS[1][0]), (3, PAIRS[1][1])]
        EMBED, EMBED_BANK = [PAIRS[0][0], PAIRS[0][1], tiles(1)], (2, 1, 3)
        FINAL, FINAL_BANK = [tiles(0), PAIRS[1][0], PAIRS[1][1]], (7, 7, 2)

        def pair_columns(n):
            ts = EMBED[n]
            return slice(ts[0] % TH // 2 * T, (ts[-1] % TH + 1) // 2 * T)

        SUMMED = (EP, EP - 2)
        STEPS = [(h, p) for h in range(HALVES) for p in range(EP)]
        ACT_ODD = (0, 1, 3, 5, 6, 7, 9, 11, 13)

        def pool_sums(k):
            return sum(0 < p < SUMMED[h] for h, p in STEPS[:k + 1])

        def act_hidden(k):
            return k + 1 + sum(s <= k for s in ACT_ODD)

        def dve_hidden(k):
            return k + 1 - sum(s <= k for s in ACT_ODD)

        @block.sync
        def _(sp):
            sp.dma_start(first[:, :], first_in).then_inc(ld_first, 16)
            for c in range(2):
                cols = slice(c * N // 2, (c + 1) * N // 2)
                sp.dma_start(xT[:, 0, :, cols], x_in[0][:, :, cols]).then_inc(ld_x[c], 16)
            sp.dma_start(rows[:, :], rows_in).then_inc(ld_rows, 16)
            sp.dma_start(xT[:, 1, :, :], x_in[1]).then_inc(ld_x[2], 16)
            sp.dma_start(qk_w[:, :, :, :], qk_in).then_inc(ld_qk, 16)
            sp.dma_start(sel_raw[:, :], sel_in).then_inc(ld_sel, 16)
            sp.dma_start(vo_w[:, :, :, :], vo_in).then_inc(ld_vo, 16)
            sp.dma_start(w1_raw[:, :, :], w1_in).then_inc(ld_w1, 16)
            sp.dma_start(gw_raw[:, :], gate_in).then_inc(ld_gw, 16)
            sp.dma_start(w2_sb[:, :, :], w2_in).then_inc(ld_w2, 16)
            ov = out.rearrange("b p d -> (b p) d").rearrange("(t p) d -> p t d", p=T)
            for n, ts in enumerate(FINAL[:-1]):
                sp.wait_ge(dve_out, n + 1)
                sp.dma_start(ov[:, ts[0]:ts[-1] + 1, :], span(res, ts)).then_inc(stored, 16)
            sp.wait_ge(stored, 16 * len(FINAL))

        @block.gpsimd
        def _(pool):
            nc.gpsimd.memset(idle[:, :].bitcast(mybir.dt.uint32), 0).then_inc(pool_idle, 1)
            nc.gpsimd.memset(mhalf[:, :], -0.5).then_inc(pool_half, 1)
            nc.gpsimd.memset(f32(xs[:, :, :]), 0.0).then_inc(pool_pads, 1)
            nc.gpsimd.memset(bd[:, 0, :, :, :, :], 0.0).then_inc(pool_bd, 1)

            def inverse_root(n, ts):
                pool.wait_ge(dve_var, NORMS.index((n, ts)) + 1)
                at = slice(ts[0], ts[-1] + 1)
                nc.gpsimd.tensor_tensor(rstd[:, n, at], var[:, n, at], mhalf[:, at], ALU.pow).then_inc(pool_rstd, 1)

            pool.wait_ge(pool_half, 1)
            w1_chunks = iter(range(8))

            def w1_low(n):
                for _, c in zip(range(n), w1_chunks):
                    pool.wait_ge(act_w1, c // 2 + 1)
                    r = slice(c * E // 8, (c + 1) * E // 8)
                    nc.gpsimd.tensor_tensor(w1_lo[:, r, :], w1_raw[:, r, :], f32(w1_hi[:, r, :]),
                                            ALU.subtract).then_inc(pool_w1, 1)

            def folded_low(lo, full, hi, ready, signal):
                pool.wait_ge(ready, 1)
                nc.gpsimd.tensor_tensor(lo[:, :, :, :], full[:, 0, :, :].rearrange("p h (r d) -> p h r d", d=D),
                                        f32(hi[:, :, :, :]), ALU.subtract).then_inc(signal, 1)

            for n, ts in NORMS[:5]:
                inverse_root(n, ts)
            folded_low(b_lo, vo_w, b_hi, act_b, pool_b)
            inverse_root(*NORMS[5])
            w1_low(4)
            inverse_root(2, PAIRS[0][0])
            w1_low(2)
            inverse_root(2, PAIRS[0][1])
            w1_low(2)
            inverse_root(2, tiles(1))
            for k, (h, p) in enumerate(STEPS):
                if 0 < p < SUMMED[h]:
                    pool.wait_ge(dve_part, k + 1)
                    if p > 1:
                        pool.wait_ge(pool_acc, pool_sums(k - 1))
                    nc.gpsimd.tensor_tensor(acc[:, h, :], acc[:, h, :], part[:, k % 2, :],
                                            ALU.add).then_inc(pool_acc, 1)
                if h == 1 and p == 2:
                    inverse_root(3, tiles(0))
            for ts in PAIRS[1]:
                inverse_root(3, ts)

        @block.scalar
        def _(act):
            act.wait_ge(pool_idle, 1)
            nc.scalar.activation(warm[:, :], idle[:, 0:1], ACT.Sigmoid)

            def folded_high(dst, full, bk, ready, signal):
                act.wait_ge(ready, 1)
                if full is not None:
                    nc.scalar.copy(full[:, 0, :, :], bank[bk][:, :].rearrange("p (h n) -> p h n", n=128))
                nc.scalar.copy(dst[:, :, :, :], bank[bk][:, :]).then_inc(signal, 1)

            def w1_high(c):
                act.wait_ge(ld_w1, 16)
                r = slice(c * E // 4, (c + 1) * E // 4)
                nc.scalar.copy(w1_hi[:, r, :], w1_raw[:, r, :]).then_inc(act_w1, 1)

            def high_part(dst, src, ready, count, signal, ts):
                act.wait_ge(ready, count)
                nc.scalar.copy(dst[:, ts[0]:ts[-1] + 1, 0, :], span(src, ts)).then_inc(signal, 1)

            act.wait_ge(ld_sel, 16)
            nc.scalar.copy(apart_j[:, :], sel_raw[0:2, EP * 128:EP * 128 + 128])
            nc.scalar.copy(apart_i[:, :], sel_raw[0:2, EP * 128 + 128:]).then_inc(act_sel, 1)
            for i, ts in enumerate(PAIRS[0]):
                high_part(stack, xn, dve_xn, i + 1, act_hi, ts)
            folded_high(a_hi, None, 7, pe_a, act_a)

            T_BANK = ((0, 1, 7, 6), (7, 2, 3, 5))
            U_BANK = ((2, 3, 5, 4), (7, 2, 3, 5))
            S_BANK = ((0, 1), (1, 6))

            def move_xs():
                act.wait_ge(pool_pads, 1)
                act.wait_ge(pe_xs, 1)
                nc.scalar.copy(xs[:, 0:TH * QUADS, 0:W],
                               bank[2][:, 0:N].rearrange("p (q w) -> p q w", w=W)).then_inc(act_xs, 1)

            def move_t(h):
                for p in ((0, 1, 2, 3), (0, 2))[h]:
                    act.wait_ge(pe_t, HP * h + p + 1)
                    nc.scalar.copy(tT[:, p, h * N:(h + 1) * N], bank[T_BANK[h][p]][:, 0:N]).then_inc(act_t, 1)

            def move_u(h, i):
                act.wait_ge(pe_u, TH * h + i + 1)
                nc.scalar.copy(u[:, h * TH + i, :], bank[U_BANK[h][i]][:, :]).then_inc(act_u, 1)

            def sigmoids(h, par):
                act.wait_ge(pe_s, 2 * h + par + 1)
                nc.scalar.activation(att[:, h, :, par * 2 * HP:(par + 1) * 2 * HP, :],
                                     bank[S_BANK[h][par]][:, 0:N].rearrange("p (c a w) -> p c a w", a=2 * HP, w=W),
                                     ACT.Sigmoid, scale=float(D) ** 0.5).then_inc(act_sig, 1)

            def expand(h):
                act.wait_ge(act_sig, 2 * h + 2)
                if h == 0:
                    act.wait_ge(pool_bd, 1)
                else:
                    act.wait_ge(dve_zero, 1)
                for tp, q in ((0, 0), (0, 1), (1, 0)):
                    r = slice(q * PAD, (q + 1) * PAD)
                    nc.scalar.copy(bd[r, h, tp, :, q, :], att[r, h, tp, :, :]).then_inc(act_bd, 1)

            def move_av(n):
                act.wait_ge(pe_av, n + 1)
                h, at = EMBED[n][0] // TH, pair_columns(n)
                nc.scalar.activation(oT[:, h, at], bank[h][:, at], ACT.Relu).then_inc(act_oT, 1)

            def move_xs2(h):
                act.wait_ge(pe_xs2, h + 1)
                nc.scalar.copy(xs2[:, h * N:(h + 1) * N], bank[(0, 7)[h]][:, 0:N]).then_inc(act_xs2, 1)

            def gate_weights(h):
                act.wait_ge(dve_gap, h + 1)
                nc.scalar.activation(gap[:, h, 1, :], gap[:, h, 0, :], ACT.Sigmoid, scale=-1.0)
                nc.scalar.activation(gap[:, h, 2, :], gap[:, h, 0, :], ACT.Sigmoid).then_inc(act_top, 1)

            move_xs()
            folded_high(b_hi, vo_w, 5, pe_b, act_b)
            move_t(0)
            move_u(0, 0)
            move_u(0, 1)
            high_part(stack, xn, dve_xn, 3, act_hi, tiles(1))
            move_u(0, 2)
            w1_high(0)
            w1_high(1)
            sigmoids(0, 0)
            sigmoids(0, 1)
            expand(0)
            move_t(1)
            move_av(0)
            move_u(1, 0)
            w1_high(2)
            sigmoids(1, 0)
            high_part(stack2, xn2, dve_xn2, 1, act_hi2, PAIRS[0][0])
            sigmoids(1, 1)
            expand(1)
            move_av(1)
            move_u(1, 2)
            move_u(1, 3)
            act.wait_ge(ld_gw, 16)
            nc.scalar.copy(gw[:, 0, :], gw_raw[:, :]).then_inc(act_gw, 1)
            nc.scalar.copy(sel[:, :], sel_raw[:, 0:EP * 128]).then_inc(act_sel, 1)

            def move_gT(h):
                act.wait_ge(pe_gT, h + 1)
                nc.scalar.copy(gT[:, h * N:(h + 1) * N], bank[(6, 7)[h]][0:2 * E, 0:N]).then_inc(act_gT, 1)

            def hidden(k):
                h, p = STEPS[k]
                for i in range(2 if k in ACT_ODD else 1):
                    act.wait_ge(pe_z, 2 * k + i + 1)
                    if k >= 2:
                        act.wait_ge(pe_o, k - 1)
                    nc.scalar.activation(h1e[:, k % 2, i, :], bank[2 - 2 * (k % 2) + i][:, 0:N], ACT.Relu,
                                         bias=b12T[:, 2 * p + i:2 * p + i + 1]).then_inc(act_z, 1)

            def move_gates(k):
                act.wait_ge(pe_g, k + 1)
                if k >= 2:
                    act.wait_ge(dve_part, k - 1)
                nc.scalar.copy(gbc[:, k % 2, :], bank[6][:, 0:N]).then_inc(act_g, 1)

            w1_high(3)
            high_part(stack2, xn2, dve_xn2, 2, act_hi2, PAIRS[0][1])
            move_xs2(0)
            move_av(2)
            hidden(0)
            gate_weights(0)
            hidden(1)
            hidden(2)
            move_gT(0)
            move_gates(0)
            for k in range(3, len(STEPS)):
                hidden(k)
                if k == 3:
                    move_gates(1)
                move_gates(max(k - 1, 2))
                if k == 3:
                    high_part(stack2, xn2, dve_xn2, 3, act_hi2, tiles(1))
                if k == 4:
                    move_xs2(1)
                if k == 6:
                    gate_weights(1)
                if k == 8:
                    move_gT(1)
            move_gates(len(STEPS) - 1)
            ts = FINAL[-1]
            act.wait_ge(dve_out, len(FINAL))
            act.dma_start(out.rearrange("b p d -> (b p) d").rearrange("(t p) d -> p t d", p=T)[:, ts[0]:ts[-1] + 1, :],
                          span(res, ts)).then_inc(stored, 16)

        @block.vector
        def _(dve):
            made = [0]

            def link(ins):
                made[0] += 1
                ins.then_inc(dve_link, 1)
                dve.wait_ge(dve_link, made[0])

            def bcast(row):
                return row.unsqueeze(1).broadcast_to([T, TH, row.shape[-1]])

            def wide(col, n):
                return col.unsqueeze(2).broadcast_to([T, col.shape[-1], n])

            def moments(n, src, ts):
                for t in ts:
                    last = nc.vector.bn_stats(stats[:, n, t, :], src(t))
                link(last)
                for t in ts:
                    last = nc.vector.bn_aggr(mv[:, n, t, :], stats[:, n, t, :])
                link(last)
                at = slice(ts[0], ts[-1] + 1)
                nc.vector.tensor_scalar(var[:, n, at], mv[:, n, at, 1], EPS, None, ALU.add).then_inc(dve_var, 1)

            def centre(n, src, ts):
                return nc.vector.tensor_tensor(span(dev, ts), src, wide(mv[:, n, ts[0]:ts[-1] + 1, 0], D),
                                               ALU.subtract)

            def centre_scaled(n, src, gamma, ts):
                for t in ts:
                    last = nc.vector.scalar_tensor_tensor(out=dev[:, t, :], in0=src(t), scalar=mv[:, n, t, 0:1],
                                                          in1=gamma, op0=ALU.subtract, op1=ALU.mult)
                return last

            def normalise(n, dst, ts):
                dve.wait_ge(pool_rstd, NORMS.index((n, ts)) + 1)
                return nc.vector.tensor_tensor(span(dst, ts), span(dev, ts), wide(rstd[:, n, ts[0]:ts[-1] + 1], D),
                                               ALU.mult)

            def normalise_add(n, dst, addend, ts):
                dve.wait_ge(pool_rstd, NORMS.index((n, ts)) + 1)
                for t in ts:
                    last = nc.vector.scalar_tensor_tensor(out=dst[:, t, :], in0=dev[:, t, :],
                                                          scalar=rstd[:, n, t:t + 1], in1=addend(t),
                                                          op0=ALU.mult, op1=ALU.add)
                return last

            def bank_tile(bk):
                return lambda t: bank[bk][0:T, t % TH * D:(t % TH + 1) * D]

            def bank_half(bk):
                return bank[bk][0:T, 0:TH * D].rearrange("p (t d) -> p t d", d=D)

            nc.vector.memset(ones[:, :], 1.0).then_inc(dve_ones, 1)
            nc.vector.memset(bd[:, 1, :, :, :, :], 0.0).then_inc(dve_zero, 1)
            dve.wait_ge(ld_rows, 16)
            nc.vector.tensor_copy(fold[:, :, :], idup.unsqueeze(1).broadcast_to([128, 2, D])).then_inc(dve_fold, 1)


            def embed_moments(i):
                dve.wait_ge(pe_y, i + 1)
                moments(0, bank_tile(EMBED_BANK[i]), EMBED[i])

            def embed_centre(i):
                centre_scaled(0, bank_tile(EMBED_BANK[i]), tokg, EMBED[i]).then_inc(dve_y, 1)

            def embed_norm(i):
                dve.wait_ge(dve_y, i + 1)
                normalise_add(0, h0, lambda t: tokbe, EMBED[i]).then_inc(dve_h0, 1)

            def second_moments(i):
                dve.wait_ge(dve_h0, i + 1)
                moments(1, lambda t: h0[:, t, :], EMBED[i])

            def second_centre(i):
                centre(1, span(h0, EMBED[i]), EMBED[i]).then_inc(dve_dev, 1)

            def second_norm(i):
                dve.wait_ge(dve_dev, i + 1)
                normalise(1, xn, EMBED[i]).then_inc(dve_xn, 1)

            def folded_low(lo, hi, bk, ready, signal):
                dve.wait_ge(ready, 1)
                nc.vector.tensor_tensor(lo[:, :, :, :], bank[bk][:, :], f32(hi[:, :, :, :]),
                                        ALU.subtract).then_inc(signal, 1)

            def low(dst, src, high, ready, count, signal, ts):
                dve.wait_ge(high, count)
                dve.wait_ge(ready, count)
                at = slice(ts[0], ts[-1] + 1)
                nc.vector.tensor_tensor(dst[:, at, 1, :], span(src, ts), f32(dst[:, at, 0, :]),
                                        ALU.subtract).then_inc(signal, 1)

            embed_moments(0)
            embed_centre(0)
            embed_moments(1)
            embed_norm(0)
            embed_centre(1)
            second_moments(0)
            embed_norm(1)
            second_centre(0)
            second_moments(1)
            second_norm(0)
            second_centre(1)
            second_norm(1)
            low(stack, xn, act_hi, dve_xn, 1, dve_lo, EMBED[0])
            low(stack, xn, act_hi, dve_xn, 2, dve_lo, EMBED[1])
            embed_moments(2)
            folded_low(a_lo, a_hi, 7, act_a, dve_a)
            embed_centre(2)
            embed_norm(2)
            second_moments(2)
            second_centre(2)

            T_BANK = ((0, 1, 7, 6), (7, 2, 3, 5))
            U_BANK = ((2, 3, 5, 4), (7, 2, 3, 5))

            def move_xs():
                dve.wait_ge(pool_pads, 1)
                dve.wait_ge(pe_xs, 2)
                nc.vector.tensor_copy(xs[:, TH * QUADS:2 * TH * QUADS, 0:W],
                                      bank[6][:, 0:N].rearrange("p (q w) -> p q w", w=W)).then_inc(dve_xs, 1)

            def move_xff(h):
                dve.wait_ge(pe_xff, h + 1)
                nc.vector.tensor_copy(xff[:, h * TH * QUADS:(h + 1) * TH * QUADS, :],
                                      bank[4][:, :]).then_inc(dve_xff, 1)

            def move_t(h):
                for p in ((), (1, 3))[h]:
                    dve.wait_ge(pe_t, HP * h + p + 1)
                    nc.vector.tensor_copy(tT[:, p, h * N:(h + 1) * N], bank[T_BANK[h][p]][:, 0:N]).then_inc(dve_t, 1)

            def move_u(h, i):
                dve.wait_ge(pe_u, TH * h + i + 1)
                nc.vector.tensor_copy(u[:, h * TH + i, :], bank[U_BANK[h][i]][:, :]).then_inc(dve_u, 1)

            def expand(h):
                dve.wait_ge(act_sig, 2 * h + 2)
                if h == 0:
                    dve.wait_ge(pool_bd, 1)
                for tp, q in ((0, 2), (0, 3), (1, 1), (1, 2), (1, 3)):
                    r = slice(q * PAD, (q + 1) * PAD)
                    nc.vector.tensor_copy(bd[r, h, tp, :, q, :], att[r, h, tp, :, :]).then_inc(dve_bd, 1)

            def residual_moments(n):
                dve.wait_ge(pe_oT, n + 1)
                ts, src = EMBED[n], bank_half(7 if n == 2 else 4)
                nc.vector.tensor_tensor(span(h1b, ts), src[:, ts[0] % TH:ts[-1] % TH + 1, :], span(h0, ts),
                                        ALU.add).then_inc(dve_h1, 1)
                dve.wait_ge(dve_h1, n + 1)
                moments(2, lambda t: h1b[:, t, :], ts)

            def residual_centre(n):
                link(centre(2, span(h1b, EMBED[n]), EMBED[n]))

            def add_beta(h):
                nc.vector.tensor_tensor(half(h1b, h), half(h1b, h), bcast(ffnbe), ALU.add).then_inc(dve_h1b, 1)
                dve.wait_ge(dve_h1b, h + 1)

            def third_norm(n):
                normalise(2, xn2, EMBED[n]).then_inc(dve_xn2, 1)

            def gates(h):
                dve.wait_ge(pe_lg, h + 1)
                both = bank[(6, 7)[h]][0:T, 0:TH * 2 * E].rearrange("p (t w e) -> p t w e", w=2, e=E)
                link(nc.vector.tensor_tensor(lg[:, h, :, :], both[:, :, 0, :], bcast(gateb), ALU.add))
                nc.vector.tensor_tensor(lg[:, h, :, :], lg[:, h, :, :], both[:, :, 1, :],
                                        ALU.add).then_inc(dve_lg, 1)
                dve.wait_ge(dve_lg, h + 1)
                for i in range(TH):
                    last = nc.vector.max(top8[:, h, i, :], lg[:, h, i, :])
                link(last)
                nc.vector.tensor_tensor(gap[:, h, 0, :], top8[:, h, :, 1], top8[:, h, :, 0],
                                        ALU.subtract).then_inc(dve_gap, 1)
                for i in range(TH):
                    last = nc.vector.max_index(at8[:, h, i, :], top8[:, h, i, :], lg[:, h, i, :])
                link(last)

            def spread_gates(h):
                nc.vector.tensor_tensor(one1[:, h, :, :], bcast(ids), wide(at8[:, h, :, 0], E), ALU.is_equal)
                link(nc.vector.tensor_tensor(one2[:, h, :, :], bcast(ids), wide(at8[:, h, :, 1], E), ALU.is_equal))
                dve.wait_ge(act_top, h + 1)
                nc.vector.tensor_tensor(one1[:, h, :, :], one1[:, h, :, :], wide(gap[:, h, 1, :], E), ALU.mult)
                link(nc.vector.tensor_tensor(one2[:, h, :, :], one2[:, h, :, :], wide(gap[:, h, 2, :], E), ALU.mult))
                link(nc.vector.tensor_tensor(g[:, h, :, :], one1[:, h, :, :], one2[:, h, :, :], ALU.add))
                link(nc.vector.tensor_copy(gs[:, h, :, 0:E], g[:, h, :, :]))
                nc.vector.tensor_tensor(gs[:, h, :, E:2 * E], g[:, h, :, :], f32(gs[:, h, :, 0:E]),
                                        ALU.subtract).then_inc(dve_gate, 1)

            def gated(k):
                h, p = STEPS[k]
                dve.wait_ge(pe_o, k + 1)
                dve.wait_ge(act_g, k + 1)
                dst = part[:, k % 2, :] if p else acc[:, h, :]
                if p and k > 2:
                    dve.wait_ge(pool_acc, pool_sums(k - 2))
                nc.vector.scalar_tensor_tensor(out=dst, in0=bank[4 + k % 2][:, 0:N],
                                               scalar=b12T[:, E + p:E + p + 1], in1=gbc[:, k % 2, :],
                                               op0=ALU.add, op1=ALU.mult).then_inc(dve_part, 1)

            def hidden(k):
                h, p = STEPS[k]
                dve.wait_ge(pe_z, 2 * k + 2)
                if k >= 2:
                    dve.wait_ge(pe_o, k - 1)
                nc.vector.tensor_scalar(h1e[:, k % 2, 1, :], bank[3 - 2 * (k % 2)][:, 0:N],
                                        b12T[:, 2 * p + 1:2 * p + 2], 0.0, ALU.add, ALU.max).then_inc(dve_z, 1)

            def finish_moments(i):
                dve.wait_ge(pe_fin, i + 1)
                src = bank_tile(FINAL_BANK[i])
                if i == 0:
                    link(nc.vector.tensor_tensor(half(res, 0), bank_half(FINAL_BANK[i]), half(xn2, 0), ALU.add))
                    src = lambda t: res[:, t, :]
                moments(3, src, FINAL[i])
                centre_scaled(3, src, ffng, FINAL[i]).then_inc(dve_fin, 1)

            def finish(i):
                dve.wait_ge(dve_fin, i + 1)
                normalise_add(3, res, lambda t: h1b[:, t, :], FINAL[i]).then_inc(dve_out, 1)

            move_xff(0)
            second_norm(2)
            low(stack, xn, act_hi, dve_xn, 3, dve_lo, EMBED[2])
            move_u(0, 3)
            move_xs()
            expand(0)
            move_t(1)
            move_xff(1)
            move_u(1, 1)
            residual_moments(0)
            residual_centre(0)
            third_norm(0)
            low(stack2, xn2, act_hi2, dve_xn2, 1, dve_lo2, PAIRS[0][0])
            expand(1)
            residual_moments(1)
            residual_centre(1)
            dve.wait_ge(act_gw, 1)
            nc.vector.tensor_tensor(gw[:, 1, :], gw_raw[:, :], f32(gw[:, 0, :]), ALU.subtract).then_inc(dve_gw, 1)
            third_norm(1)
            low(stack2, xn2, act_hi2, dve_xn2, 2, dve_lo2, PAIRS[0][1])
            add_beta(0)
            gates(0)
            spread_gates(0)
            residual_moments(2)
            hidden(2)
            gated(0)
            residual_centre(2)
            add_beta(1)
            gated(1)
            third_norm(2)
            for k in range(3, len(STEPS)):
                if k not in ACT_ODD:
                    hidden(k)
                gated(k - 1)
                if k == 3:
                    low(stack2, xn2, act_hi2, dve_xn2, 3, dve_lo2, tiles(1))
                if k == 5:
                    gates(1)
                if k == 6:
                    spread_gates(1)
                if k == 10:
                    finish_moments(0)
                if k == 12:
                    finish(0)
            dve.wait_ge(pool_acc, pool_sums(len(STEPS) - 1))
            dve.wait_ge(dve_part, len(STEPS) - 1)
            nc.vector.tensor_tensor(acc[:, 1, :], acc[:, 1, :], part[:, 0, :], ALU.add).then_inc(dve_acc, 1)
            gated(len(STEPS) - 1)
            finish_moments(1)
            finish_moments(2)
            finish(1)
            finish(2)

        @block.tensor
        def _(pe):
            mm = nc.tensor.matmul

            def keep_warm(n, bk=5):
                for _ in range(n):
                    mm(bank[bk][:, :], idle[:, :], idle[:, :].unsqueeze(1).broadcast_to([128, 4, 128]),
                       start=True, stop=True)

            pe.wait_ge(pool_idle, 1)
            keep_warm(6)
            pe.wait_ge(ld_first, 16)
            pe.wait_ge(dve_ones, 1)

            def embed(n):
                ts, bk = EMBED[n], bank[EMBED_BANK[n]]
                mm(bk[0:T, ts[0] % TH * D:(ts[-1] % TH + 1) * D], ones[:, :], tokb[:, 0:len(ts), :],
                   start=True, stop=True)
                pe.wait_ge(ld_x[n], 16)
                for t in ts:
                    h, i = t // TH, t % TH
                    for c in range(2):
                        last = mm(bk[0:T, i * D:(i + 1) * D], xT[:, h, c, i * T:(i + 1) * T], tokwT[:, c, :],
                                  start=False, stop=(c == 1), skip_group_check=True)
                last.then_inc(pe_y, 1)

            def fold_weights(w, bk, loaded, signal):
                pe.wait_ge(loaded, 16)
                for p in range(HP):
                    last = mm(bank[bk][:, p * 128:(p + 1) * 128], w[:, 0, p, :], w[:, 1, p, :], start=True, stop=True)
                last.then_inc(signal, 1)

            for n in range(len(EMBED)):
                embed(n)
            fold_weights(qk_w, 7, ld_qk, pe_a)
            keep_warm(1, 0)

            def features_first(h, bk):
                pe.wait_ge(dve_lo, 2 + h)
                for i, t in enumerate(tiles(h)):
                    last = nc.tensor.transpose(bank[bk][:, i * T:(i + 1) * T], f32(stack[:, t, :, :]),
                                               ident[0:T, 0:T])
                last.then_inc(pe_xs, 1)

            def rejoin(h):
                mm(bank[4][:, :], fold[:, :, :], xs[:, h * TH * QUADS:(h + 1) * TH * QUADS, :],
                   start=True, stop=True).then_inc(pe_xff, 1)

            def queries(h, p, bk):
                rhs = xs[:, h * TH * QUADS:(h + 1) * TH * QUADS, 0:W]
                mm(bank[bk][:, 0:N], a_hi[:, p, :, :], rhs, start=True, stop=False)
                mm(bank[bk][:, 0:N], a_lo[:, p, :, :], rhs, start=False, stop=True).then_inc(pe_t, 1)

            def values(t, bk):
                lhs = xs[:, t * QUADS:(t + 1) * QUADS, :]
                mm(bank[bk][:, :], lhs, b_hi[:, :, :, :], start=True, stop=False)
                mm(bank[bk][:, :], lhs, b_lo[:, :, :, :], start=False, stop=True).then_inc(pe_u, 1)

            def scores(h, par, bk):
                r = slice(par * D, (par + 1) * D)
                mm(bank[bk][:, 0:N], apart_j[:, :], apart_i[:, :], start=True, stop=True)
                for i, t in enumerate(tiles(h)):
                    for q in range(QUADS):
                        at = t * T + q * W
                        last = mm(bank[bk][q * PAD:(q + 1) * PAD, i * HP * W:(i + 1) * HP * W],
                                  xff[r, t * QUADS + q, :], tT[r, :, at:at + W], start=False, stop=True,
                                  skip_group_check=True, tile_position=(par * D, q * PAD))
                last.then_inc(pe_s, 1)

            def attend(h, tp, heads=range(H)):
                pe.wait_ge(act_bd, 3 * h + (2, 3)[tp])
                pe.wait_ge(dve_bd, 5 * h + (2, 5)[tp])
                for hd in heads:
                    for i in range(2):
                        t = 2 * tp + i
                        row = ((hd % 2) * 2 + i) * HP + hd // 2
                        last = mm(bank[h][i * D:(i + 1) * D, tp * T:(tp + 1) * T],
                                  u[:, h * TH + t, hd * D:(hd + 1) * D],
                                  bd[:, h, tp, row, :, :], start=(hd == 0), stop=(hd == H - 1))
                if (h == 0 or tp == TH // 2 - 1) and heads[-1] == H - 1:
                    last.then_inc(pe_av, 1)

            def tokens_first(n, bk):
                pe.wait_ge(act_oT, n + 1)
                h, ts = EMBED[n][0] // TH, EMBED[n]
                for tp in range(ts[0] % TH // 2, (ts[-1] % TH + 1) // 2):
                    last = nc.tensor.transpose(bank[bk][0:T, tp * 128:(tp + 1) * 128],
                                               oT[:, h, tp * T:(tp + 1) * T], ident)
                last.then_inc(pe_oT, 1)

            def features_first2(h, bk):
                pe.wait_ge(dve_lo2, h + 2)
                for i, t in enumerate(tiles(h)):
                    last = nc.tensor.transpose(bank[bk][:, i * T:(i + 1) * T], f32(stack2[:, t, :, :]),
                                               ident[0:T, 0:T])
                last.then_inc(pe_xs2, 1)

            def gate_logits(h, bk):
                pe.wait_ge(act_xs2, h + 1)
                for i, t in enumerate(tiles(h)):
                    last = mm(bank[bk][0:T, i * 2 * E:(i + 1) * 2 * E], xs2[:, t * T:(t + 1) * T], gw[:, :, :],
                              start=True, stop=True)
                last.then_inc(pe_lg, 1)

            pe.wait_ge(dve_y, 2)
            features_first(0, 2)
            fold_weights(vo_w, 5, ld_vo, pe_b)
            pe.wait_ge(dve_a, 1)
            pe.wait_ge(act_xs, 1)
            queries(0, 0, 0)
            queries(0, 1, 1)
            queries(0, 2, 7)
            queries(0, 3, 6)
            pe.wait_ge(dve_fold, 1)
            rejoin(0)
            pe.wait_ge(pool_b, 1)
            pe.wait_ge(dve_y, 3)
            for i, bk in ((0, 2), (1, 3), (2, 5)):
                values(i, bk)
            pe.wait_ge(dve_xff, 1)
            values(3, 4)
            pe.wait_ge(act_t, 4)
            pe.wait_ge(act_sel, 1)
            scores(0, 0, 0)
            features_first(1, 6)
            scores(0, 1, 1)
            pe.wait_ge(act_u, 3)
            pe.wait_ge(dve_u, 1)
            pe.wait_ge(dve_xs, 1)
            for p, bk in enumerate((7, 2, 3, 5)):
                queries(1, p, bk)
            rejoin(1)
            attend(0, 0)
            pe.wait_ge(act_t, 5)
            values(TH, 7)
            pe.wait_ge(dve_t, 1)
            values(TH + 1, 2)
            pe.wait_ge(dve_xff, 2)
            tokens_first(0, 4)
            pe.wait_ge(act_t, 6)
            pe.wait_ge(dve_t, 2)
            scores(1, 0, 1)
            scores(1, 1, 6)
            attend(0, 1)
            values(TH + 2, 3)
            values(TH + 3, 5)
            pe.wait_ge(dve_h1, 1)
            tokens_first(1, 4)
            pe.wait_ge(act_u, 4)
            pe.wait_ge(dve_u, 2)
            attend(1, 0)
            pe.wait_ge(act_u, 6)
            attend(1, 1, range(6))
            features_first2(0, 0)
            attend(1, 1, range(6, H))
            pe.wait_ge(dve_gw, 1)
            gate_logits(0, 6)

            def layer1(k):
                h, p = STEPS[k]
                if h == 0:
                    pe.wait_ge(pool_w1, p + 1)
                if k >= 2:
                    pe.wait_ge(act_z, act_hidden(k - 2))
                    if dve_hidden(k - 2):
                        pe.wait_ge(dve_z, dve_hidden(k - 2))
                for i in range(2):
                    z = bank[2 - 2 * (k % 2) + i][:, 0:N]
                    rhs = xs2[:, h * N:(h + 1) * N]
                    mm(z, w1_hi[:, 2 * p + i, :], rhs, start=True, stop=False)
                    mm(z, w1_lo[:, 2 * p + i, :], rhs, start=False, stop=True).then_inc(pe_z, 1)

            def spread(k):
                h, p = STEPS[k]
                pe.wait_ge(act_gT, h + 1)
                if k:
                    pe.wait_ge(act_g, k)
                mm(bank[6][:, 0:N], sel[:, p * 128:(p + 1) * 128], gT[:, h * N:(h + 1) * N],
                   start=True, stop=True).then_inc(pe_g, 1)

            def layer2(k):
                h, p = STEPS[k]
                pe.wait_ge(act_z, act_hidden(k))
                if dve_hidden(k):
                    pe.wait_ge(dve_z, dve_hidden(k))
                if k >= 2:
                    pe.wait_ge(dve_part, k - 1)
                for i in range(2):
                    last = mm(bank[4 + k % 2][i * D:(i + 1) * D, 0:N], w2_sb[:, 2 * p + i, :], h1e[:, k % 2, i, :],
                              start=True, stop=True)
                last.then_inc(pe_o, 1)

            def gates_first(h, bk):
                pe.wait_ge(dve_gate, h + 1)
                for i in range(TH):
                    last = nc.tensor.transpose(bank[bk][0:2 * E, i * T:(i + 1) * T], f32(gs[:, h, i, :]),
                                               ident[0:T, 0:T])
                last.then_inc(pe_gT, 1)

            def collect(h):
                sums = [(acc[:, h, :], *((pool_acc, pool_sums(EP - 1)) if h == 0 else (dve_acc, 1)))]
                for p in range(EP - h, EP):
                    k = h * EP + p
                    sums.append((part[:, k % 2, :], dve_part, k + 1))
                parts = [n for n, ts in enumerate(FINAL) if ts[0] // TH == h]
                for n in parts if h else ():
                    ts = FINAL[n]
                    mm(bank[FINAL_BANK[n]][0:T, ts[0] % TH * D:(ts[-1] % TH + 1) * D], ident[0:T, 0:T],
                       span(xn2, ts), start=True, stop=True)
                for j, (src, ready, count) in enumerate(sums):
                    pe.wait_ge(ready, count)
                    for n in parts:
                        for t in FINAL[n]:
                            i = t % TH
                            last = mm(bank[FINAL_BANK[n]][0:T, i * D:(i + 1) * D], src[:, i * T:(i + 1) * T], idup,
                                      start=(h == 0), stop=True, skip_group_check=True)
                        if j == len(sums) - 1:
                            last.then_inc(pe_fin, 1)

            pe.wait_ge(act_oT, 3)
            pe.wait_ge(ld_w2, 16)
            layer1(0)
            tokens_first(2, 7)
            layer1(1)
            layer2(0)
            layer1(2)
            gates_first(0, 6)
            layer2(1)
            spread(0)
            for k in range(3, len(STEPS)):
                layer1(k)
                if k == 3:
                    spread(1)
                    layer2(2)
                    spread(2)
                else:
                    spread(k - 1)
                    layer2(k - 1)
                if k == 4:
                    features_first2(1, 7)
                if k == 5:
                    gate_logits(1, 7)
                if k == 8:
                    gates_first(1, 7)
                if k == 10:
                    pe.wait_ge(act_gT, 2)
                    collect(0)
            spread(len(STEPS) - 1)
            layer2(len(STEPS) - 1)
            pe.wait_ge(dve_fin, 1)
            collect(1)


def kernel(**inputs):
    import numpy as _np
    import concourse.bacc as _bacc
    from concourse import mybir as _mybir
    from concourse.bass_utils import run_bass_kernel_spmd as _run

    v = {n.removeprefix("L0_"): _np.asarray(a) for n, a in inputs.items()}
    f4 = _np.float32

    def spread_rows(a, n=128):
        return _np.broadcast_to(a[None, :], (n, a.shape[0]))

    def by_pair(a):
        return a.reshape(-1, D, HP, 2).transpose(3, 1, 2, 0).reshape(128, HP, -1)

    rows = v["x"].reshape(B, S * FEAT)[:, :Q * C].reshape(B, Q, C)
    patches = _np.stack([rows[:, c:c + P] for c in range(2)])
    x_in = patches.reshape(2, HALVES, N, C).transpose(1, 3, 0, 2)
    first = _np.concatenate([v["tok_W"].reshape(D, 2, C).transpose(2, 1, 0).reshape(C, 2 * D),
                             _np.eye(128, dtype=f4), spread_rows(v["tok_b"])], axis=1)
    idup = _np.tile(_np.eye(D, dtype=f4), (2, 1))
    b2_pairs = v["ffn_b2"].reshape(EP, 2 * D).T
    rows_in = _np.concatenate(
        [spread_rows(v[n]) for n in ("tok_gamma", "tok_beta", "ffn_gamma", "ffn_beta", "ffn_gate_b")]
        + [spread_rows(_np.arange(E, dtype=f4)), idup, v["ffn_b1"].T, b2_pairs], axis=1)

    def block_diagonal(a):
        out = _np.zeros((2, D, HP, 2, D), f4)
        for par in range(2):
            out[par, :, :, par, :] = a.reshape(2, D, HP, D)[par]
        return out.reshape(128, HP, 128)

    wo = v["attn_Wo"].reshape(D, HP, 2, D).transpose(2, 0, 1, 3).reshape(128, HP, D)
    qk_in = _np.stack([_np.tile(by_pair(v["attn_Wq"]), (1, 1, 2)), block_diagonal(by_pair(v["attn_Wk"]))], axis=1)
    vo_in = _np.stack([_np.tile(by_pair(v["attn_Wv"]), (1, 1, 2)), block_diagonal(wo)], axis=1)
    w1_in = _np.tile(v["ffn_w1"].transpose(1, 0, 2), (2, 1, 1))
    w2_in = v["ffn_w2"].transpose(1, 0, 2)
    gate_in = _np.tile(v["ffn_gate_w"], (2, 1))
    sel_in = _np.zeros((2 * E, EP * 128 + 128 + N), f4)
    k = _np.arange(2 * E)[:, None, None] % E
    pair, col = _np.arange(EP)[None, :, None], _np.arange(128)[None, None, :]
    sel_in[:, :EP * 128] = (k == 2 * pair + col // D).reshape(2 * E, EP * 128)
    clip, j, i = _np.arange(2)[:, None], _np.arange(128)[None, :] % PAD, _np.arange(N)[None, :] % W
    sel_in[0:2, EP * 128:EP * 128 + 128] = (j // P == clip) & (j < W)
    sel_in[0:2, EP * 128 + 128:] = _np.where(i // P == clip, 0.0, APART)

    nc = _bacc.Bacc("TRN2", target_bir_lowering=False, num_devices=1)
    arrays, args = {}, []
    for name, a in (("x", x_in), ("first", first), ("rows", rows_in), ("qk", qk_in), ("vo", vo_in), ("w1", w1_in),
                    ("w2", w2_in), ("gate", gate_in), ("sel", sel_in)):
        a = _np.ascontiguousarray(a)
        arrays[f"in_{name}_dram"] = a
        args.append(nc.dram_tensor(f"in_{name}_dram", a.shape, _mybir.dt.from_np(a.dtype), kind="ExternalInput").ap())
    out = nc.dram_tensor("out_dram", (B, P, D), _mybir.dt.float32, kind="ExternalOutput").ap()
    audio_tower(nc, *args, out)
    res = _run(nc, [arrays], core_ids=[0])
    return res.results[0]["out_dram"]
```
